# Optimizing a Trainium2 kernel written in Bass

```python
import numpy as np
import jax
import jax.numpy as jnp

def _softmax(x, axis=-1):
    return jax.nn.softmax(x, axis=axis)

def _gelu(x):
    return jax.nn.gelu(x, approximate=True)

def _silu(x):
    return jax.nn.silu(x)

def _sigmoid(x):
    return jax.nn.sigmoid(x)

def _layernorm(x, axis=-1, eps=1e-05):
    m = jnp.mean(x, axis=axis, keepdims=True)
    v = jnp.var(x, axis=axis, keepdims=True)
    return (x - m) / jnp.sqrt(v + eps)

def _scatter_add(tgt, idx, src, axis=0):
    return tgt.at[idx].add(src)

def _segment_sum(src, seg, n):
    return jax.ops.segment_sum(src, seg, n)
kernel_name = 'mk_adaln_ffn_d1_seqx_r4_b1276e'

def setup_inputs(seed: int=0):
    np.random.seed(seed)
    _w = jnp.asarray

    def _rec_inputs():
        import jax
        import jax.numpy as jnp
        _rk = jax.random.key(seed)
        x = -0.000125 + 0.9999 * jax.random.normal(jax.random.fold_in(_rk, 1), (4, 512, 512), jnp.float32)
        _lenS = 512 - jax.random.randint(jax.random.fold_in(_rk, 7), (4,), 0, max(1, 512 // 4) + 1, jnp.int32)
        _lenS2 = 512 - jax.random.randint(jax.random.fold_in(_rk, 8), (4,), 0, max(1, 512 // 4) + 1, jnp.int32)
        fside_BxSxS_0 = -1.52775e-05 + 0.999936 * jax.random.normal(jax.random.fold_in(_rk, 11), (4, 512, 512), jnp.float32)
        cond_512 = -5.03954e-05 + 1.00559 * jax.random.normal(jax.random.fold_in(_rk, 12), (4, 128), jnp.float32)
        return (x, fside_BxSxS_0, cond_512)
    x, fside_BxSxS_0, cond_512 = _rec_inputs()

    def _L0_cond_setup():
        import jax, jax.numpy as jnp
        from jax import lax
        import numpy as np
        B, T, C, TD = (8, 512, 512, 128)

        def _bi_wkv(r, k, v, w, u, time_emb):
            tf = jax.nn.sigmoid(jnp.sum(time_emb, axis=-1))[:, None, None]
            decay = jnp.exp(-jnp.exp(w.astype(jnp.float32)))[None, :] * (0.5 + 0.5 * tf[:, :, 0])
            kf = k.astype(jnp.float32)
            vf = v.astype(jnp.float32)
            ek = jnp.exp(jnp.minimum(kf, 30.0))
            ekv = ek * vf

            def step(carry, x):
                a, b = carry
                ekv_t, ek_t = x
                a = a * decay + ekv_t
                b = b * decay + ek_t
                return ((a, b), (a, b))
            ekv_t = jnp.swapaxes(ekv, 0, 1)
            ek_t = jnp.swapaxes(ek, 0, 1)
            init = (jnp.zeros_like(decay), jnp.zeros_like(decay))
            _, (nf, df) = lax.scan(step, init, (ekv_t, ek_t))
            _, (nb, db) = lax.scan(step, init, (ekv_t, ek_t), reverse=True)
            nf = jnp.swapaxes(nf, 0, 1)
            df = jnp.swapaxes(df, 0, 1)
            nb = jnp.swapaxes(nb, 0, 1)
            db = jnp.swapaxes(db, 0, 1)
            euk = jnp.exp(jnp.minimum(u.astype(jnp.float32)[None, None, :] + kf, 30.0))
            num = nf + nb - ekv + euk * vf
            den = df + db - ek + euk
            base = jax.nn.sigmoid(r.astype(jnp.float32)) * (num / jnp.maximum(den, 1e-08))
            out = base * (0.8 + 0.2 * tf)
            return out.astype(r.dtype)
        key = jax.random.key(seed)
        ks = jax.random.split(key, 6)
        return {'r': jax.random.normal(ks[0], (B, T, C), dtype=jnp.float32), 'k': jax.random.normal(ks[1], (B, T, C), dtype=jnp.float32), 'v': jax.random.normal(ks[2], (B, T, C), dtype=jnp.float32), 'w': jax.random.normal(ks[3], (C,), dtype=jnp.float32), 'u': jax.random.normal(ks[4], (C,), dtype=jnp.float32), 'time_emb': jax.random.normal(ks[5], (B, TD), dtype=jnp.float32)}
    _L0_cond_all = _L0_cond_setup()
    _L0_cond_in = {k: v for k, v in _L0_cond_all.items() if k in ('w', 'u')}
    del _L0_cond_all

    def _L0_ffn_setup():
        import jax, jax.numpy as jnp
        import numpy as np
        E = 32
        G = 8
        TKG = 4
        K = 4
        D = 512
        H = 256
        HS = 1024
        SCALE = 2.5
        CAP = 256

        def relu2(x):
            r = jnp.maximum(x, 0.0)
            return r * r

        def route_tokens(scores, bias_corr):
            T = scores.shape[0]
            scores_c = scores + bias_corr
            group_scores = jax.lax.top_k(scores_c.reshape(T, G, E // G), 2)[0].sum(-1)
            _, group_idx = jax.lax.top_k(group_scores, TKG)
            group_mask = jnp.zeros((T, G), scores.dtype).at[jnp.arange(T)[:, None], group_idx].set(1.0)
            score_mask = jnp.repeat(group_mask, E // G, axis=1)
            masked = jnp.where(score_mask > 0, scores_c, 0.0)
            _, topk_idx = jax.lax.top_k(masked, K)
            topk_w = jnp.take_along_axis(scores, topk_idx, axis=1)
            topk_w = topk_w / (topk_w.sum(-1, keepdims=True) + 1e-20)
            return (topk_idx, topk_w * SCALE)
        key = jax.random.key(seed)
        ks = jax.random.split(key, 6)
        B, S = (2, 512)
        return dict(hidden_states=jax.random.normal(ks[0], (B, S, D), jnp.float32), gate_w=jax.random.normal(ks[1], (E, D), jnp.float32) * 0.02, bias_corr=jnp.zeros((E,), jnp.float32), up_w=jax.random.normal(ks[2], (E, H, D), jnp.float32) * 0.02, down_w=jax.random.normal(ks[3], (E, D, H), jnp.float32) * 0.02, shared_up_w=jax.random.normal(ks[4], (HS, D), jnp.float32) * 0.02, shared_down_w=jax.random.normal(ks[5], (D, HS), jnp.float32) * 0.02)
    _L0_ffn_all = _L0_ffn_setup()
    _L0_ffn_in = {k: v for k, v in _L0_ffn_all.items() if k in ('gate_w', 'bias_corr', 'up_w', 'down_w', 'shared_up_w', 'shared_down_w')}
    del _L0_ffn_all
    return {'x': x, 'fside_BxSxS_0': fside_BxSxS_0, 'cond_512': cond_512, 'L0_cond_w': _L0_cond_in['w'], 'L0_cond_u': _L0_cond_in['u'], 'L0_ffn_gate_w': _L0_ffn_in['gate_w'], 'L0_ffn_bias_corr': _L0_ffn_in['bias_corr'], 'L0_ffn_up_w': _L0_ffn_in['up_w'], 'L0_ffn_down_w': _L0_ffn_in['down_w'], 'L0_ffn_shared_up_w': _L0_ffn_in['shared_up_w'], 'L0_ffn_shared_down_w': _L0_ffn_in['shared_down_w']}

def reference(x, fside_BxSxS_0, cond_512, L0_cond_w, L0_cond_u, L0_ffn_gate_w, L0_ffn_bias_corr, L0_ffn_up_w, L0_ffn_down_w, L0_ffn_shared_up_w, L0_ffn_shared_down_w):
    import jax
    import jax.numpy as jnp

    def _L0_cond_ref(r, k, v, w, u, time_emb):
        import jax, jax.numpy as jnp
        from jax import lax
        import numpy as np
        B, T, C, TD = (8, 512, 512, 128)

        def _bi_wkv(r, k, v, w, u, time_emb):
            tf = jax.nn.sigmoid(jnp.sum(time_emb, axis=-1))[:, None, None]
            decay = jnp.exp(-jnp.exp(w.astype(jnp.float32)))[None, :] * (0.5 + 0.5 * tf[:, :, 0])
            kf = k.astype(jnp.float32)
            vf = v.astype(jnp.float32)
            ek = jnp.exp(jnp.minimum(kf, 30.0))
            ekv = ek * vf

            def step(carry, x):
                a, b = carry
                ekv_t, ek_t = x
                a = a * decay + ekv_t
                b = b * decay + ek_t
                return ((a, b), (a, b))
            ekv_t = jnp.swapaxes(ekv, 0, 1)
            ek_t = jnp.swapaxes(ek, 0, 1)
            init = (jnp.zeros_like(decay), jnp.zeros_like(decay))
            _, (nf, df) = lax.scan(step, init, (ekv_t, ek_t))
            _, (nb, db) = lax.scan(step, init, (ekv_t, ek_t), reverse=True)
            nf = jnp.swapaxes(nf, 0, 1)
            df = jnp.swapaxes(df, 0, 1)
            nb = jnp.swapaxes(nb, 0, 1)
            db = jnp.swapaxes(db, 0, 1)
            euk = jnp.exp(jnp.minimum(u.astype(jnp.float32)[None, None, :] + kf, 30.0))
            num = nf + nb - ekv + euk * vf
            den = df + db - ek + euk
            base = jax.nn.sigmoid(r.astype(jnp.float32)) * (num / jnp.maximum(den, 1e-08))
            out = base * (0.8 + 0.2 * tf)
            return out.astype(r.dtype)
        return _bi_wkv(r, k, v, w, u, time_emb)

    def _L0_ffn_ref(hidden_states, gate_w, bias_corr, up_w, down_w, shared_up_w, shared_down_w):
        import jax, jax.numpy as jnp
        import numpy as np
        E = 32
        G = 8
        TKG = 4
        K = 4
        D = 512
        H = 256
        HS = 1024
        SCALE = 2.5
        CAP = 256

        def relu2(x):
            r = jnp.maximum(x, 0.0)
            return r * r

        def route_tokens(scores, bias_corr):
            T = scores.shape[0]
            scores_c = scores + bias_corr
            group_scores = jax.lax.top_k(scores_c.reshape(T, G, E // G), 2)[0].sum(-1)
            _, group_idx = jax.lax.top_k(group_scores, TKG)
            group_mask = jnp.zeros((T, G), scores.dtype).at[jnp.arange(T)[:, None], group_idx].set(1.0)
            score_mask = jnp.repeat(group_mask, E // G, axis=1)
            masked = jnp.where(score_mask > 0, scores_c, 0.0)
            _, topk_idx = jax.lax.top_k(masked, K)
            topk_w = jnp.take_along_axis(scores, topk_idx, axis=1)
            topk_w = topk_w / (topk_w.sum(-1, keepdims=True) + 1e-20)
            return (topk_idx, topk_w * SCALE)
        B, S, _ = hidden_states.shape
        T = B * S
        flat = hidden_states.reshape(T, D)
        logits = flat @ gate_w.T
        scores = jax.nn.sigmoid(logits)
        topk_idx, topk_w = route_tokens(scores, bias_corr)
        e_flat = topk_idx.reshape(-1)
        oh = jax.nn.one_hot(e_flat, E, dtype=jnp.int32)
        pos = jnp.take_along_axis(jnp.cumsum(oh, axis=0) - 1, e_flat[:, None], axis=1)[:, 0]
        tok = jnp.repeat(jnp.arange(T), K)
        valid = pos < CAP
        xe = jnp.zeros((E, CAP, D), flat.dtype).at[e_flat, pos].set(flat[tok], mode='drop')
        h = relu2(jnp.einsum('ecd,ehd->ech', xe, up_w))
        ye = jnp.einsum('ech,edh->ecd', h, down_w)
        gathered = ye[e_flat, jnp.minimum(pos, CAP - 1)]
        gathered = jnp.where(valid[:, None], gathered, 0.0) * topk_w.reshape(-1)[:, None]
        routed = gathered.reshape(T, K, D).sum(axis=1).reshape(B, S, D)
        shared = relu2(hidden_states @ shared_up_w.T) @ shared_down_w.T
        return routed + shared
    x = x + _L0_ffn_ref(_L0_cond_ref(x, fside_BxSxS_0, fside_BxSxS_0, L0_cond_w, L0_cond_u, cond_512), L0_ffn_gate_w, L0_ffn_bias_corr, L0_ffn_up_w, L0_ffn_down_w, L0_ffn_shared_up_w, L0_ffn_shared_down_w)
    return x

_drawn_inputs = setup_inputs


def setup_inputs(seed=0):
    import zlib

    import numpy as np

    out = dict(_drawn_inputs(seed))
    spreads = {'L0_ffn_bias_corr': (0.0, 0.427)}
    factors = {'cond_512': 8.0,
     'L0_cond_w': 3.073,
     'L0_cond_u': 8.0,
     'L0_ffn_gate_w': 6.184,
     'L0_ffn_up_w': 5.127,
     'L0_ffn_down_w': 4.673,
     'L0_ffn_shared_up_w': 3.335,
     'L0_ffn_shared_down_w': 3.129}
    for name, (base, spread) in spreads.items():
        noise = np.random.default_rng([zlib.crc32(name.encode()), seed]).standard_normal(out[name].shape)
        drawn = base * np.exp(spread * noise) if base else spread * noise
        out[name] = jnp.asarray(drawn.astype(out[name].dtype))
    for name, factor in factors.items():
        out[name] = (out[name] * factor).astype(out[name].dtype)
    return out
```

```python
from contextlib import ExitStack

import concourse.bass as bass
from concourse import mybir
from concourse.alu_op_type import AluOpType as ALU

FP = mybir.dt.float32
FR = mybir.dt.float32r
F16 = mybir.dt.float16
I32 = mybir.dt.int32
U32 = mybir.dt.uint32
ACT = mybir.ActivationFunctionType
AX = mybir.AxisListType

B, T, C = 4, 512, 512
NTOK = B * T
TD = 128
E, G, TKG, K, H = 32, 8, 4, 4, 256
EG = E // G
HS = 1024
CAP = 256
SCALE = 2.5
P = 128
NC = C // P
NI = T // P
NJ = HS // P
NH = H // P
NS = CAP // P
SA, SB = CAP // 16, 16
EL = P // SA
NG = E // EL
ROW = C + E
KLIM = 30.0
RAW = 4


def adaln_moe_kernel(nc, xT, kT, xrow, cond, wdec, ubon, gateT, bias, upT, downT, supT, sdownT, out):
    rows = nc.dram_tensor("token_rows", [NTOK, ROW], FP, kind="Internal").ap()

    ctx = ExitStack()
    with ctx:
        def sb(name, shape, dt=FP):
            return ctx.enter_context(nc.sbuf_tensor(name, shape, dt))

        def sem(name):
            return ctx.enter_context(nc.semaphore(name))

        work = sb("work", [P, 19, T])
        kt = [work[:, n, :] for n in (0, 1)]
        er = [work[:, n, :] for n in (2, 3, 18)]
        ek = [work[:, n, :] for n in (4, 5)]
        eu = [work[:, n, :] for n in (6, 7)]
        ekv = [work[:, n, :] for n in (8, 9)]
        dv = [work[:, n, :] for n in (10, 11)]
        num = [work[:, n, :] for n in (12, 13)]
        den = [work[:, n, :] for n in (14, 15)]
        nb, db = work[:, 16, :], work[:, 17, :]
        raw = work[:, 0:16, :].rearrange("p (s n) t -> p s (n t)", s=RAW)
        pool = sb("flat_or_gathered", [P, RAW * NS * ROW])
        fT = pool[:, 0:2 * NC * T].rearrange("p (b c t) -> p b c t", b=2, c=NC)
        xe = pool[:, :].rearrange("p (s h r) -> p s h r", s=RAW, h=NS)
        parts = [sb(f"parts{n}", [P, 2, NC * T], FR) for n in (0, 1)]
        flat_hi = [x[:, 0, :].rearrange("p (c t) -> p c t", c=NC) for x in parts]
        flat_lo = [x[:, 1, :].rearrange("p (c t) -> p c t", c=NC) for x in parts]
        UPW = NC * H
        DNW = NH * C
        sup = [sb(f"shared_up{n}", [P, NC, HS], FR) for n in (0, 1)]
        sdn = [sb(f"shared_down{n}", [P, NJ, C], FR) for n in (0, 1)]
        xt_even = [sb(f"xt{n}", [P, NC, CAP], FR) for n in (0, 1)]
        xt = [xt_even, [x[:, 0, :].rearrange("p (c s) -> p c s", c=NC) for x in sup]]
        hr = sb("h_relu", [P, T])
        hq = sb("h_square", [P, 2, T])
        hh = sb("h_hi", [P, 3, T], FR)
        hl = sb("h_lo", [P, 3, T], FR)
        yb = sb("y", [P, 4, C])
        rowb = sb("rows_out", [P, 2, C])
        gate = sb("gate", [P, NC, E])
        biasb = sb("bias_all", [P, E])
        dec = sb("decay", [P, B, NC])
        wcol = sb("w_col", [P, NC])
        ucol = sb("u_col", [P, NC])
        tf = sb("tf", [P, B])
        tfd = sb("tf_decay", [P, B])
        tfs = sb("tf_scale", [P, B])
        ident = sb("ident", [P, P])
        lower = sb("before", [P, P], F16)
        ones = sb("ones", [P, P], F16)
        iota = sb("iota", [P, E])
        tid = sb("token_id", [P, B * NI])
        blk = sb("blk_mask", [P, EL])
        low8 = sb("low_mask", [P, NS, 8])
        low = sb("low_sum", [P, 8])
        sel = sb("sel", [P, EL, NS], F16)
        slot = sb("dummy_row", [P, NS])
        ex = sb("r_exp", [P, NI, E])
        sc = sb("r_score", [P, NI, E])
        scb = sb("r_biased", [P, NI, E])
        pmx = sb("r_pair_max", [P, NI * G, 2])
        pmn = sb("r_pair_min", [P, NI * G, 2])
        gs = sb("r_group", [P, NI * G])
        g1 = sb("r_group1", [P, NI * G])
        g2 = sb("r_group2", [P, NI * G])
        top = sb("r_top", [P, NI, 8])
        tix = sb("r_top_index", [P, NI, 8], U32)
        geq = sb("r_group_eq", [P, NI, TKG, G])
        eeq = sb("r_expert_eq", [P, NI, K, E], F16)
        mcnt = sb("r_mask_count", [P, E])
        gmask = sb("r_group_mask", [P, NI, G])
        mask = sb("r_mask", [P, NI, E])
        mask16 = sb("r_mask16", [P, NI, E], F16)
        msum = sb("r_mask_sum", [P, 2, E], F16)
        wsel = sb("r_weight", [P, NI, E])
        wsum = sb("r_weight_sum", [P, NI])
        pint = sb("r_slot", [P, NI, E], I32)
        pa = scb[:, :, :].bitcast(I32)
        pbt = sc[:, :, :].bitcast(I32)
        pa16 = sb("r_slot_a16", [P, NI, E], F16)
        pb16 = sb("r_slot_b16", [P, NI, E], F16)
        oa = sb("onehot_a", [P, NI, NG, SA * EL], F16)
        ob = sb("onehot_b", [P, NI, NG, SB * EL], F16)
        iota16 = sb("iota16", [P, SA, EL], F16)
        tval = db[:, 0:NS * E]
        tgat = sb("t_gather", [P, NS * E], I32)
        tscat = sb("t_scatter", [P, NS * E], I32)
        tzero = db[:, NS * E:2 * NS * E]
        blkbig = nb.rearrange("p (g b e) -> p g b e", g=NG, e=EL)
        dblk = db[:, 2 * NS * E:2 * NS * E + NG * SB].rearrange("p (g b) -> p g b", g=NG)
        lsel = oa[:, 0, :, :].rearrange("p g (a b) -> p g a b", a=8)
        gi = sb("gather_index", [P, 2, NS], I32)
        si = sb("scatter_index", [P, 2, NS], I32)
        wx = sb("slot_weight", [P, RAW, NS])

        bank = [ctx.enter_context(nc.psum_tensor(f"bank{n}", [P, T], FP)) for n in range(8)]
        acc, ring, misc, idxb = bank[0:4], bank[4:6], bank[6], bank[7]
        ybank, tbank = bank[0:2], bank[6:8]

        s_const, s_gate, s_cond, s_cst = sem("s_const"), sem("s_gate"), sem("s_cond"), sem("s_cst")
        s_k = [sem("s_k0"), sem("s_k1")]
        s_r = [sem("s_r0"), sem("s_r1"), sem("s_r2")]
        s_stage = [sem("s_stage0"), sem("s_stage1")]
        s_swh, s_swl = sem("s_shared_hi"), sem("s_shared_lo")
        s_vec = sem("s_vector_chain")
        s_dexp, s_tfe, s_act = sem("s_decay_exp"), sem("s_tf_exp"), sem("s_scalar_chain")
        s_neg, s_dec = sem("s_tf_neg"), sem("s_decay")
        s_clamp, s_ek, s_eu, s_er = sem("s_clamped"), sem("s_ek"), sem("s_eu"), sem("s_er")
        s_ekv, s_du, s_dv = sem("s_ekv"), sem("s_du"), sem("s_dv")
        s_den, s_rcp = sem("s_den"), sem("s_reciprocal")
        s_flat, s_fhi, s_flo = sem("s_flat"), sem("s_flat_hi"), sem("s_flat_lo")
        s_full, s_free = sem("s_ring_full"), sem("s_ring_free")
        s_rowe, s_rowd = sem("s_row_copied"), [sem("s_row_stored0"), sem("s_row_stored1")]
        s_lg, s_lgx = sem("s_logits"), sem("s_logits_exp")
        s_mask, s_w, s_wst = sem("s_mask"), sem("s_weights"), sem("s_weights_stored")
        s_pos, s_pint, s_oh, s_idx = sem("s_pos"), sem("s_pos_read"), sem("s_onehot"), sem("s_idx")
        s_lsel, s_sel, s_tab = sem("s_lsel"), sem("s_sel"), sem("s_table")
        s_sq, s_hh, s_hl, s_dn = sem("s_square"), sem("s_h_hi"), sem("s_h_lo"), sem("s_down")
        s_acc, s_accf = sem("s_acc"), sem("s_acc_copied")
        s_xr = [sem("s_xrow0"), sem("s_xrow1")]
        s_yx, s_out = sem("s_y_plus_x"), [sem("s_out0"), sem("s_out1")]
        s_zero, s_zst = sem("s_zero"), sem("s_zero_stored")
        s_raw = [sem(f"s_raw{n}") for n in range(RAW)]
        s_xg = [sem(f"s_gathered{n}") for n in range(RAW)]
        s_uph, s_upl, s_dnh, s_dnl = sem("s_up_hi"), sem("s_up_lo"), sem("s_down_hi"), sem("s_down_lo")
        s_tr, s_thi, s_tlo, s_wx = sem("s_transposed"), sem("s_xt_hi"), sem("s_xt_lo"), sem("s_slot_weight")
        s_esq, s_ehh, s_ehl = sem("s_e_square"), sem("s_e_hi"), sem("s_e_lo")
        s_yd, s_y = sem("s_y_done"), sem("s_y_scaled")
        s_sc = [sem("s_scattered0"), sem("s_scattered1")]
        s_ix = sem("s_index_copied")
        s_go = sem("s_pair_may_go")

        NT = B * NC
        NROW = NI + NJ
        NCH = 8
        CH = HS
        PER = RAW
        SPLIT_AT = {0: (0, 1), 1: (2,), 2: (3,), 3: (4,), 4: (5,), 5: (6,), 6: (7,)}

        def wait(eng, s, v):
            if not isinstance(v, int) or v > 0:
                eng.wait_ge(s, v)

        def chunk(parts_, q):
            up, dn = parts_
            return up[:, q, :] if q < NC else dn[:, 2 * (q - NC):2 * (q - NC) + 2, :].rearrange("p j c -> p (j c)")

        def staging(q):
            return yb[:, 2 * (q % 2):2 * (q % 2) + 2, :].rearrange("p a c -> p (a c)")

        def turns(eng, step):
            for e in range(-1, PER):
                step(e, e // PER, e % PER)
            with eng.Fori(1, E // PER - 1) as i:
                for u in range(PER):
                    step(i * PER + u, i, u)
            for e in range(E - PER, E + 1):
                step(e, e // PER, e % PER)

        def has(e, d):
            return not isinstance(e, int) or 0 <= e + d < E

        block = ctx.enter_context(nc.Block())

        @block.sync
        def _(sp):
            def load_tile(n):
                b, c = divmod(n, NC)
                if n >= 2:
                    sp.wait_ge(s_dv, n - 1)
                sp.dma_start(kt[n % 2], kT[c * P:(c + 1) * P, b, :]).then_inc(s_k[n % 2], 16)
                if n >= 3:
                    sp.wait_ge(s_flat, n - 2)
                sp.dma_start(er[n % 3], xT[c * P:(c + 1) * P, b, :]).then_inc(s_r[n % 3], 16)

            def load_stage(q):
                if q >= 2:
                    sp.wait_ge(s_swl, q - 1)
                src = supT[:, q, :] if q < NC else sdownT[:, 2 * (q - NC):2 * (q - NC) + 2, :].rearrange("p j c -> p (j c)")
                sp.dma_start(staging(q), src).then_inc(s_stage[q % 2], 16)

            sp.dma_start(wcol[:, :], wdec).then_inc(s_const, 16)
            sp.dma_start(ucol[:, :], ubon).then_inc(s_const, 16)
            sp.dma_start(rowb[:, 0, :], cond.rearrange("b t -> (b t)").partition_broadcast(P)).then_inc(s_cond, 16)
            load_tile(0)
            load_tile(1)
            sp.dma_start(gate[:, :, :], gateT).then_inc(s_gate, 16)
            sp.dma_start(biasb[:, :], bias.partition_broadcast(P)).then_inc(s_gate, 16)
            for q in range(2):
                load_stage(q)
            for s in range(B + 1):
                for c in range(NC):
                    n = NC * s + c + 2
                    if n < NT:
                        load_tile(n)
                    for q in SPLIT_AT.get(n - 2, ()):
                        if q + 2 < NCH:
                            load_stage(q + 2)
                if s == 0:
                    sp.wait_ge(s_zero, 1)
                    sp.dma_start(out[NTOK:NTOK + CAP, :].rearrange("(h p) c -> p h c", h=NS),
                                 hq[:, :, :]).then_inc(s_zst, 16)
                if s >= 1:
                    for i in range(NI):
                        t = NI * (s - 1) + i
                        if t == 0:
                            sp.wait_ge(s_swl, NCH)
                        if t >= 2:
                            sp.wait_ge(s_yx, t - 1)
                        sp.dma_start(yb[:, 2 + t % 2, :], xrow[t * P:(t + 1) * P, :]).then_inc(s_xr[t % 2], 16)
                        if i >= 1:
                            store_out = t - 1
                            sp.wait_ge(s_yx, store_out + 1)
                            sp.dma_start(out[store_out * P:(store_out + 1) * P, :], yb[:, store_out % 2, :]).then_inc(s_out[store_out % 2], 16)
                    t = NI * s - 1
                    sp.wait_ge(s_yx, t + 1)
                    sp.dma_start(out[t * P:(t + 1) * P, :], yb[:, t % 2, :]).then_inc(s_out[t % 2], 16)

                if s == B - 1:
                    sp.wait_ge(s_flat, NT)
                    for e in range(RAW):
                        sp.dma_start(raw[:, e, 0:UPW], upT[e]).then_inc(s_raw[e], 16)
                        sp.dma_start(raw[:, e, UPW:UPW + DNW], downT[e]).then_inc(s_raw[e], 16)

            with sp.Fori(1, E // RAW) as i:
                for u in range(RAW):
                    sp.wait_ge(s_upl, i * RAW + (u - RAW + 1))
                    sp.dma_start(raw[:, u, 0:UPW], upT[bass.ds(i * RAW + u, 1)].rearrange("o p n -> (o p) n")).then_inc(s_raw[u], 16)
                    sp.wait_ge(s_dnl, i * RAW + (u - RAW + 1))
                    sp.dma_start(raw[:, u, UPW:UPW + DNW], downT[bass.ds(i * RAW + u, 1)].rearrange("o p n -> (o p) n")).then_inc(s_raw[u], 16)

        @block.tensor
        def _(pe):
            def three(dst, lhs, rhs, first, last):
                pe.matmul(dst, lhs[0], rhs[0], start=first, stop=False)
                pe.matmul(dst, lhs[0], rhs[1], start=False, stop=False)
                return pe.matmul(dst, lhs[1], rhs[0], start=False, stop=last)

            def turn_rows(b):
                pe.wait_ge(s_flat, NC * (b + 1))
                if b == 0:
                    pe.wait_ge(s_cst, 1)
                for i in range(NI):
                    m = NROW * b + i
                    wait(pe, s_free, m - 1)
                    for c in range(NC):
                        ins = pe.transpose(ring[m % 2][:, c * P:(c + 1) * P], fT[:, b % 2, c, i * P:(i + 1) * P], ident[:, :])
                    ins.then_inc(s_full, 1)
                    if i == 0:
                        if b == 0:
                            pe.wait_ge(s_gate, 32)
                        else:
                            pe.wait_ge(s_pint, b)
                    for c in range(NC):
                        ins = pe.matmul(misc[:, i * E:(i + 1) * E], fT[:, b % 2, c, i * P:(i + 1) * P], gate[:, c, :],
                                        start=c == 0, stop=c == NC - 1)
                ins.then_inc(s_lg, 1)

            def up(b, j):
                m = NROW * b + NI + j
                if j == 0:
                    pe.wait_ge(s_flo, NC * (b + 1))
                    if b == 0:
                        pe.wait_ge(s_swl, NC)
                pe.wait_ge(s_free, m - 1)
                for c in range(NC):
                    ins = three(ring[m % 2][:, :], [w[:, c, j * P:(j + 1) * P] for w in sup],
                                [flat_hi[b % 2][:, c, :], flat_lo[b % 2][:, c, :]], c == 0, c == NC - 1)
                ins.then_inc(s_full, 1)

            def down(b, j):
                J = NJ * b + j
                pe.wait_ge(s_hl, J + 1)
                if b == 0 and j % 2 == 0:
                    pe.wait_ge(s_swl, NC + j // 2 + 1)
                for i in range(NI):
                    if j == 0:
                        wait(pe, s_accf, NI * (b - 1) + i + 1)
                    ins = three(acc[i][:, :], [h[:, J % 3, i * P:(i + 1) * P] for h in (hh, hl)],
                                [w[:, j, :] for w in sdn], j == 0, j == NJ - 1)
                    if j == NJ - 1:
                        ins.then_inc(s_acc, 1)
                if j < NJ - 1:
                    ins.then_inc(s_dn, 1)

            def positions(b):
                pe.wait_ge(s_mask, b + 1)
                for i in range(NI):
                    dst = misc[:, P + i * E:P + (i + 1) * E]
                    pe.matmul(dst, lower[:, :], mask16[:, i, :], start=True, stop=False)
                    for before in range(i):
                        pe.matmul(dst, ones[:, :], mask16[:, before, :], start=False, stop=False)
                    ins = pe.matmul(dst, ones[:, :], msum[:, b % 2, :], start=False, stop=True)
                ins.then_inc(s_pos, 1)

            def places(b):
                pe.wait_ge(s_oh, b + 1)
                for i in range(NI):
                    for g in range(NG):
                        first, last = b == 0 and i == 0 and g == 0, b == B - 1 and i == NI - 1
                        ins = pe.matmul(idxb[:, g * P:(g + 1) * P],
                                        oa[:, i, g, :], ob[:, i, g, :],
                                        start=first, stop=last and g == NG - 1, skip_group_check=True)
                ins.then_inc(s_idx, 1)

            def table():
                pe.wait_ge(s_lsel, 1)
                for g in range(NG):
                    ins = pe.matmul(misc[:, 2 * P + g * 2 * EL:2 * P + (g + 1) * 2 * EL],
                                    lsel[:, g, :, :].rearrange("p a b -> p (a b)"), sel[:, :, :].rearrange("p e h -> p (e h)"), start=True, stop=True)
                ins.then_inc(s_sel, 1)

            def turn_expert(e, i, u):
                pe.wait_ge(s_xg[u], (i + 1) * 32)
                if isinstance(e, int) and e == 0:
                    pe.wait_ge(s_tab, 1)
                for n in range(2):
                    wait(pe, s_thi, 2 * (e - 1) + n + 1)
                    wait(pe, s_tlo, 2 * (e - 1) + n + 1)
                    for c in (2 * n, 2 * n + 1):
                        for h in range(NS):
                            o = (c % 2) * CAP + h * P
                            ins = pe.transpose(tbank[n][:, o:o + P], xe[:, u, h, c * P:(c + 1) * P], ident[:, :])
                    ins.then_inc(s_tr, 1)

            def expert_weights(u, dn):
                if dn:
                    return [parts[u % 2][:, x, UPW:UPW + DNW].rearrange("p (h c) -> p h c", h=NH) for x in (0, 1)]
                return [parts[u % 2][:, x, 0:UPW].rearrange("p (c h) -> p c h", c=NC) for x in (0, 1)]

            def expert_up(e, u):
                pe.wait_ge(s_tlo, 2 * e + 2)
                pe.wait_ge(s_upl, e + 1)
                pe.wait_ge(s_free, NROW * B + e - 1)
                w = expert_weights(u, False)
                for hb in range(NH):
                    for c in range(NC):
                        ins = three(ring[u % 2][:, hb * CAP:(hb + 1) * CAP], [x[:, c, hb * P:(hb + 1) * P] for x in w],
                                    [x[:, c, :] for x in xt[u % 2]], c == 0, c == NC - 1)
                ins.then_inc(s_full, 1)

            def expert_down(e, u):
                pe.wait_ge(s_ehl, e + 1)
                pe.wait_ge(s_dnl, e + 1)
                w = expert_weights(u, True)
                for h in range(NS):
                    if isinstance(e, int) and e == 0:
                        pe.wait_ge(s_accf, NI * B)
                    wait(pe, s_y, 2 * (e - 1) + h + 1)
                    for hb in range(NH):
                        ins = three(ybank[h][:, :], [x[:, u % 2, hb * CAP + h * P:hb * CAP + (h + 1) * P] for x in (hh, hl)],
                                    [x[:, hb, :] for x in w], hb == 0, hb == NH - 1)
                    ins.then_inc(s_yd, 1)

            for b in range(B):
                turn_rows(b)
                if b >= 1:
                    places(b - 1)
                up(b, 0)
                up(b, 1)
                for j in range(NJ):
                    if j + 2 < NJ:
                        up(b, j + 2)
                    down(b, j)
                    if b < B - 1 and j == 5:
                        positions(b)
                    if b == B - 1:
                        if j == 0:
                            positions(b)
                        if j == 2:
                            places(b)
                        if j == 3:
                            table()

            def step(e, i, u):
                if has(e, 1):
                    turn_expert(e + 1, i + (u + 1) // PER, (u + 1) % PER)
                if has(e, 0):
                    expert_up(e, u)
                if has(e, -1):
                    expert_down(e - 1, (u - 1) % PER)

            turns(pe, step)

        @block.scalar
        def _(act):
            chain = [0]

            def link(ins):
                chain[0] += 1
                ins.then_inc(s_act, 1)
                return chain[0]

            act.preload_act_table_set("natural_log_exp_and_others")
            act.wait_ge(s_const, 32)
            act.wait_ge(s_act, link(act.activation(wcol[:, :], wcol[:, :], ACT.Exp)))
            act.activation(wcol[:, :], wcol[:, :], ACT.Exp, scale=-1.0).then_inc(s_dexp, 1)
            act.wait_ge(s_neg, 1)
            act.activation(tf[:, :], tf[:, :], ACT.Exp).then_inc(s_tfe, 1)

            def exps(n):
                act.wait_ge(s_clamp, 2 * n + 1)
                act.activation(ek[n % 2], ek[n % 2], ACT.Exp).then_inc(s_ek, 1)
                act.wait_ge(s_clamp, 2 * n + 2)
                act.activation(eu[n % 2], eu[n % 2], ACT.Exp).then_inc(s_eu, 1)
                act.wait_ge(s_r[n % 3], 16 * (n // 3 + 1))
                act.wait_ge(s_act, link(act.activation(er[n % 3], er[n % 3], ACT.Exp, scale=-1.0)))
                act.activation(er[n % 3], er[n % 3], ACT.Copy, bias=1.0).then_inc(s_er, 1)

            def reciprocal(n):
                act.wait_ge(s_den, n + 1)
                act.wait_ge(s_act, link(act.activation(er[n % 3], den[n % 2], ACT.Ln)))
                act.activation(er[n % 3], er[n % 3], ACT.Exp, scale=-1.0).then_inc(s_rcp, 1)

            def flat_high(n):
                b, c = divmod(n, NC)
                act.wait_ge(s_flat, n + 1)
                if b >= 2:
                    act.wait_ge(s_full, NROW * (b - 1))
                act.activation(flat_hi[b % 2][:, c, :], fT[:, b % 2, c, :], ACT.Copy).then_inc(s_fhi, 1)

            def shared_weights_high(q):
                act.wait_ge(s_stage[q % 2], 16 * (q // 2 + 1))
                act.activation(chunk((sup[0], sdn[0]), q), staging(q), ACT.Copy).then_inc(s_swh, 1)

            def post(J):
                b, j = divmod(J, NJ)
                act.wait_ge(s_full, NROW * b + NI + j + 1)
                wait(act, s_sq, J)
                act.activation(hr[:, :], ring[j % 2][:, :], ACT.Relu).then_inc(s_free, 1)
                act.wait_ge(s_free, NROW * b + NI + j + 1)
                wait(act, s_hl, J - 1)
                if J == 0:
                    act.wait_ge(s_zst, 16)
                act.activation(hq[:, J % 2, :], hr[:, :], ACT.Square).then_inc(s_sq, 1)
                act.wait_ge(s_sq, J + 1)
                if J >= 3:
                    last = J - 3
                    if last % NJ == NJ - 1:
                        act.wait_ge(s_acc, NI * (last // NJ + 1))
                    else:
                        act.wait_ge(s_dn, last - last // NJ + 1)
                act.activation(hh[:, J % 3, :], hq[:, J % 2, :], ACT.Copy).then_inc(s_hh, 1)

            def sums_out(b):
                for i in range(NI):
                    t = NI * b + i
                    act.wait_ge(s_acc, t + 1)
                    if t >= 2:
                        act.wait_ge(s_out[t % 2], 16 * (t // 2))
                    else:
                        act.wait_ge(s_swl, NCH)
                    act.activation(yb[:, t % 2, :], acc[i][:, :], ACT.Copy).then_inc(s_accf, 1)

            def rows_out(b):
                for i in range(NI):
                    t = NI * b + i
                    act.wait_ge(s_full, NROW * b + i + 1)
                    if t >= 2:
                        act.wait_ge(s_rowd[t % 2], 16 * (t // 2))
                    elif t == 0:
                        act.wait_ge(s_neg, 1)
                    act.activation(rowb[:, t % 2, :], ring[i % 2][:, :], ACT.Copy).then_inc(s_free, 1)
                    act.wait_ge(s_free, NROW * b + i + 1)
                    act.dma_start(rows[t * P:(t + 1) * P, 0:C], rowb[:, t % 2, :]).then_inc(s_rowd[t % 2], 16)
                act.wait_ge(s_lg, b + 1)
                if b >= 1:
                    act.wait_ge(s_mask, b)
                act.activation(ex[:, :, :].rearrange("p i e -> p (i e)"), misc[:, 0:NI * E], ACT.Exp,
                               scale=-1.0).then_inc(s_lgx, 1)

            def up_high(e, i, u):
                act.wait_ge(s_raw[u], (i + 1) * 32)
                if isinstance(e, int) and e < 2:
                    act.wait_ge(s_full, NROW * (B - 1 + e))
                else:
                    act.wait_ge(s_full, NROW * B + e - 1)
                act.activation(parts[u % 2][:, 0, 0:UPW], raw[:, u, 0:UPW], ACT.Copy).then_inc(s_uph, 1)

            def down_high(e, u):
                if not (isinstance(e, int) and e < 2):
                    act.wait_ge(s_yd, 2 * e - 2)
                act.activation(parts[u % 2][:, 0, UPW:UPW + DNW], raw[:, u, UPW:UPW + DNW], ACT.Copy).then_inc(s_dnh, 1)

            def xt_high(e, u):
                for n in range(2):
                    act.wait_ge(s_tr, 2 * e + n + 1)
                    if not (isinstance(e, int) and e == 0):
                        act.wait_ge(s_full, NROW * B + e - 1)
                    act.activation(xt[u % 2][0][:, 2 * n:2 * n + 2, :].rearrange("p c s -> p (c s)"), tbank[n][:, :],
                                   ACT.Copy).then_inc(s_thi, 1)

            def expert_square(e, u):
                act.wait_ge(s_full, NROW * B + e + 1)
                if isinstance(e, int) and e == 0:
                    act.wait_ge(s_sq, NJ * B)
                else:
                    act.wait_ge(s_esq, e)
                act.activation(hr[:, :], ring[u % 2][:, :], ACT.Relu).then_inc(s_free, 1)
                act.wait_ge(s_free, NROW * B + e + 1)
                if isinstance(e, int) and e < 2:
                    act.wait_ge(s_hl, NJ * B)
                else:
                    act.wait_ge(s_ehl, e - 1)
                act.activation(hq[:, u % 2, :], hr[:, :], ACT.Square).then_inc(s_esq, 1)

            def results(e, i, u):
                act.wait_ge(s_wx, e + 1)
                if isinstance(e, int) and e < 2:
                    act.wait_ge(s_out[0], 16 * NI * B // 2)
                    act.wait_ge(s_out[1], 16 * NI * B // 2)
                else:
                    act.wait_ge(s_sc[u % 2], (2 * i + u // 2) * 32)
                for h in range(NS):
                    act.wait_ge(s_yd, 2 * e + h + 1)
                    act.activation(yb[:, 2 * (u % 2) + h, :], ybank[h][:, :], ACT.Copy,
                                   scale=wx[:, u, h:h + 1]).then_inc(s_y, 1)

            exps(0)
            for s in range(B + 1):
                for c in range(NC):
                    n = NC * s + c
                    if n + 1 < NT:
                        exps(n + 1)
                    for q in SPLIT_AT.get(n, ()):
                        shared_weights_high(q)
                    if s >= 1 and c == 0:
                        if n < NT:
                            reciprocal(n)
                        flat_high(n - 1)
                        rows_out(s - 1)
                    if s >= 1:
                        post(NJ * (s - 1) + 2 * c)
                    if c >= 1 or s == 0:
                        if n < NT:
                            reciprocal(n)
                    if s >= 1:
                        post(NJ * (s - 1) + 2 * c + 1)
                    if c >= 1 and n < NT:
                        flat_high(n - 1)
                if s >= 1 and s < B:
                    sums_out(s - 1)

            def step(e, i, u):
                if has(e, 1):
                    up_high(e + 1, i + (u + 1) // PER, (u + 1) % PER)
                if has(e, 0):
                    down_high(e, u)
                if has(e, 1):
                    xt_high(e + 1, (u + 1) % PER)
                if has(e, 0):
                    expert_square(e, u)
                if isinstance(e, int) and e == -1:
                    sums_out(B - 1)
                if has(e, -1):
                    results(e - 1, i + (u - 1) // PER, (u - 1) % PER)

            turns(act, step)

        @block.vector
        def _(dve):
            chain = [0]

            def link(ins):
                chain[0] += 1
                ins.then_inc(s_vec, 1)
                return chain[0]

            def tt(o, a, b_, op):
                return link(dve.tensor_tensor(o, a, b_, op))

            def after(n):
                dve.wait_ge(s_vec, n)

            dve.wait_ge(s_cond, 16)
            after(link(dve.tensor_reduce(tf[:, :], rowb[:, 0, :].rearrange("p (b t) -> p b t", b=B), AX.X, ALU.add)))
            dve.tensor_scalar(tf[:, :], tf[:, :], -1.0, 80.0, ALU.mult, ALU.min).then_inc(s_neg, 1)

            def clamp(n):
                dve.wait_ge(s_k[n % 2], 16 * (n // 2 + 1))
                if n == 0:
                    dve.wait_ge(s_const, 32)
                if n >= 2:
                    dve.wait_ge(s_dv, n - 1)
                dve.tensor_scalar(ek[n % 2], kt[n % 2], KLIM, None, ALU.min).then_inc(s_clamp, 1)
                dve.tensor_scalar(eu[n % 2], kt[n % 2], ucol[:, n % NC:n % NC + 1], KLIM, ALU.add,
                                  ALU.min).then_inc(s_clamp, 1)

            clamp(0)
            dve.wait_ge(s_tfe, 1)
            after(link(dve.tensor_scalar(tf[:, :], tf[:, :], 1.0, None, ALU.add)))
            after(link(dve.reciprocal(tf[:, :], tf[:, :])))
            link(dve.tensor_scalar(tfs[:, :], tf[:, :], -0.2, -0.8, ALU.mult, ALU.add))
            after(link(dve.tensor_scalar(tfd[:, :], tf[:, :], 0.5, 0.5, ALU.mult, ALU.add)))
            dve.wait_ge(s_dexp, 1)
            for b in range(B):
                n0 = link(dve.tensor_scalar(dec[:, b, :], wcol[:, :], tfd[:, b:b + 1], None, ALU.mult))
            link(dve.memset(msum[:, 0, :], 0.0))
            after(n0)

            def wkv(n):
                b, c = divmod(n, NC)
                d = dec[:, b, c:c + 1].to_broadcast([P, T])
                e_, v_, nf, df = ek[n % 2], ekv[n % 2], num[n % 2], den[n % 2]
                if n + 1 < NT:
                    clamp(n + 1)
                if n >= 2:
                    dve.wait_ge(s_flat, n - 1)
                dve.wait_ge(s_ek, n + 1)
                a1 = link(dve.tensor_tensor_scan(df, d, e_, 0.0, ALU.mult, ALU.add))
                a2 = link(dve.tensor_tensor_scan(db[:, ::-1], d, e_[:, ::-1], 0.0, ALU.mult, ALU.add))
                dve.wait_ge(s_ekv, n + 1)
                a3 = link(dve.tensor_tensor_scan(nf, d, v_, 0.0, ALU.mult, ALU.add))
                a4 = link(dve.tensor_tensor_scan(nb[:, ::-1], d, v_[:, ::-1], 0.0, ALU.mult, ALU.add))
                after(a2)
                a5 = tt(df, df, db, ALU.add)
                after(a4)
                a6 = tt(nf, nf, nb, ALU.add)
                dve.wait_ge(s_dv, n + 1)
                after(a5)
                a7 = tt(df, df, eu[n % 2], ALU.add)
                after(a6)
                a8 = tt(nf, nf, dv[n % 2], ALU.add)
                dve.wait_ge(s_er, n + 1)
                after(a7)
                dve.scalar_tensor_tensor(out=df, in0=df, scalar=1e-8, in1=er[n % 3], op0=ALU.max, op1=ALU.mult).then_inc(s_den, 1)
                if n >= 1:
                    divide(n - 1)
                return a8

            def divide(n):
                b, c = divmod(n, NC)
                dve.wait_ge(s_rcp, n + 1)
                a1 = tt(den[n % 2], den[n % 2], er[n % 3], ALU.mult)
                a2 = link(dve.scalar_tensor_tensor(out=num[n % 2], in0=num[n % 2], scalar=tfs[:, b:b + 1], in1=er[n % 3],
                                                   op0=ALU.mult, op1=ALU.mult))
                if b >= 2:
                    dve.wait_ge(s_flo, NC * (b - 1))
                    dve.wait_ge(s_lg, b - 1)
                after(a2)
                dve.scalar_tensor_tensor(out=fT[:, b % 2, c, :], in0=den[n % 2], scalar=2.0, in1=num[n % 2],
                                         op0=ALU.subtract, op1=ALU.mult).then_inc(s_flat, 1)

            def choose(b):
                dve.wait_ge(s_lgx, b + 1)
                if b == 0:
                    dve.wait_ge(s_gate, 32)
                    dve.wait_ge(s_cst, 1)
                if b >= 1:
                    dve.wait_ge(s_wst, 16 * b)
                    dve.wait_ge(s_pos, b)
                flat = lambda x: x[:, :, :].rearrange("p i e -> p (i e)")
                after(link(dve.tensor_scalar(flat(ex), flat(ex), 1.0, None, ALU.add)))
                after(link(dve.reciprocal(flat(sc), flat(ex))))
                after(tt(scb[:, :, :], sc[:, :, :], biasb[:, None, :].to_broadcast([P, NI, E]), ALU.add))
                pair = flat(scb).rearrange("p (g q x) -> p g q x", q=2, x=2)
                tt(pmx[:, :, :], pair[:, :, :, 0], pair[:, :, :, 1], ALU.max)
                after(tt(pmn[:, :, :], pair[:, :, :, 0], pair[:, :, :, 1], ALU.min))
                tt(g1[:, :], pmx[:, :, 0], pmx[:, :, 1], ALU.min)
                tt(g2[:, :], pmn[:, :, 0], pmn[:, :, 1], ALU.max)
                after(tt(gs[:, :], pmx[:, :, 0], pmx[:, :, 1], ALU.max))
                after(tt(g1[:, :], g1[:, :], g2[:, :], ALU.max))
                after(tt(gs[:, :], gs[:, :], g1[:, :], ALU.add))
                for i in range(NI):
                    last = link(dve.max(top[:, i, :], gs[:, i * G:(i + 1) * G]))
                after(last)
                for i in range(NI):
                    last = link(dve.max_index(tix[:, i, :], top[:, i, :], gs[:, i * G:(i + 1) * G]))
                after(last)
                after(tt(geq[:, :, :, :], tix[:, :, 0:TKG][:, :, :, None].to_broadcast([P, NI, TKG, G]),
                         iota[:, 0:G][:, None, None, :].to_broadcast([P, NI, TKG, G]), ALU.is_equal))
                after(link(dve.tensor_reduce(gmask[:, :, :], geq[:, :, :, :].rearrange("p i k g -> p i g k"), AX.X, ALU.add)))
                after(tt(ex[:, :, :].rearrange("p i (g x) -> p (i g) x", x=EG), scb[:, :, :].rearrange("p i (g x) -> p (i g) x", x=EG),
                         gmask[:, :, :].rearrange("p i g -> p (i g)")[:, :, None].to_broadcast([P, NI * G, EG]), ALU.mult))
                for i in range(NI):
                    last = link(dve.max(top[:, i, :], ex[:, i, :]))
                after(last)
                for i in range(NI):
                    last = link(dve.max_index(tix[:, i, :], top[:, i, :], ex[:, i, :]))
                after(last)
                after(tt(eeq[:, :, :, :], tix[:, :, 0:K][:, :, :, None].to_broadcast([P, NI, K, E]),
                         iota[:, :][:, None, None, :].to_broadcast([P, NI, K, E]), ALU.is_equal))
                after(link(dve.tensor_reduce(mask[:, :, :], eeq[:, :, :, :].rearrange("p i k e -> p i e k"), AX.X, ALU.add)))
                last = tt(wsel[:, :, :], sc[:, :, :], mask[:, :, :], ALU.mult)
                dve.tensor_copy(mask16[:, :, :], mask[:, :, :]).then_inc(s_mask, 1)
                after(last)
                after(link(dve.tensor_reduce(wsum[:, :], wsel[:, :, :], AX.X, ALU.add)))
                if b < B - 1:
                    link(dve.tensor_reduce(mcnt[:, :], mask[:, :, :].rearrange("p i e -> p e i"), AX.X, ALU.add))
                after(link(dve.tensor_scalar(wsum[:, :], wsum[:, :], 1e-20, None, ALU.add)))
                after(link(dve.reciprocal(wsum[:, :], wsum[:, :])))
                if b < B - 1:
                    tt(msum[:, (b + 1) % 2, :], msum[:, b % 2, :], mcnt[:, :], ALU.add)
                after(tt(wsel[:, :, :], wsel[:, :, :], wsum[:, :, None].to_broadcast([P, NI, E]), ALU.mult))
                dve.tensor_scalar(wsel[:, :, :], wsel[:, :, :], SCALE, None, ALU.mult).then_inc(s_w, 1)

            def place(b):
                dve.wait_ge(s_pos, b + 1)
                if b >= 1:
                    dve.wait_ge(s_idx, b)
                pos = misc[:, P:P + NI * E].rearrange("p (i e) -> p i e", i=NI)
                dve.scalar_tensor_tensor(out=mask[:, :, :], in0=pos, scalar=1.0, in1=mask[:, :, :],
                                         op0=ALU.add, op1=ALU.mult).then_inc(s_pint, 1)
                dve.wait_ge(s_pint, b + 1)
                after(link(dve.tensor_scalar(pint[:, :, :], mask[:, :, :], 1.0, None, ALU.subtract)))
                link(dve.tensor_scalar(pa, pint[:, :, :], 4, None, ALU.arith_shift_right))
                after(link(dve.tensor_scalar(pbt, pint[:, :, :], SB - 1, None, ALU.bitwise_and)))
                link(dve.tensor_copy(pa16[:, :, :], pa))
                after(link(dve.tensor_copy(pb16[:, :, :], pbt)))
                for o, v in ((ob, pb16), (oa, pa16)):
                    for i in range(NI):
                        last = tt(o[:, i, :, :].rearrange("p g (a e) -> p g a e", a=SA),
                                  v[:, i, :].rearrange("p (g e) -> p g e", g=NG)[:, :, None, :].to_broadcast([P, NG, SA, EL]),
                                  iota16[:, None, :, :].to_broadcast([P, NG, SA, EL]), ALU.is_equal)
                for i in range(NI):
                    after(last - 2 * NI + 1 + i)
                    if i == NI - 1:
                        after(last)
                    ins = dve.tensor_scalar(ob[:, i, :, :], ob[:, i, :, :], tid[:, b * NI + i:b * NI + i + 1], None, ALU.mult)
                    if i < NI - 1:
                        link(ins)
                ins.then_inc(s_oh, 1)

            def make_table():
                dve.wait_ge(s_idx, B)
                after(tt(blkbig, idxb[:, :].rearrange("p (g b e) -> p g b e", g=NG, e=EL),
                         blk[:, None, None, :].to_broadcast([P, NG, SB, EL]), ALU.mult))
                after(link(dve.tensor_reduce(dblk, blkbig, AX.X, ALU.add)))
                dve.tensor_tensor(lsel, dblk[:, :, None, :].to_broadcast([P, NG, 8, SB]),
                                  low[:, None, :, None].to_broadcast([P, NG, 8, SB]), ALU.mult).then_inc(s_lsel, 1)
                dve.wait_ge(s_sel, 1)
                after(link(dve.tensor_copy(tval, misc[:, 2 * P:2 * P + NS * E])))
                after(link(dve.tensor_scalar(tzero, tval, 0.0, None, ALU.is_equal)))
                link(dve.tensor_scalar(tgat[:, :], tval, 1.0, 0.0, ALU.subtract, ALU.max))
                after(tt(tzero.rearrange("p (e h) -> p e h", h=NS), tzero.rearrange("p (e h) -> p e h", h=NS),
                         slot[:, None, :].to_broadcast([P, E, NS]), ALU.mult))
                dve.scalar_tensor_tensor(out=tscat[:, :], in0=tval, scalar=-1.0, in1=tzero,
                                         op0=ALU.add, op1=ALU.add).then_inc(s_tab, 1)

            for s in range(B):
                for c in range(NC):
                    wkv(NC * s + c)
                    if s >= 1 and c == 1:
                        choose(s - 1)
                if s >= 1:
                    place(s - 1)
            divide(NT - 1)
            choose(B - 1)
            place(B - 1)
            make_table()

            def up_low(e, u):
                dve.wait_ge(s_uph, e + 1)
                dve.tensor_tensor(parts[u % 2][:, 1, 0:UPW], raw[:, u, 0:UPW],
                                  parts[u % 2][:, 0, 0:UPW].bitcast(FP), ALU.subtract).then_inc(s_upl, 1)

            def down_low(e, u):
                dve.wait_ge(s_dnh, e + 1)
                dve.tensor_tensor(parts[u % 2][:, 1, UPW:UPW + DNW], raw[:, u, UPW:UPW + DNW],
                                  parts[u % 2][:, 0, UPW:UPW + DNW].bitcast(FP), ALU.subtract).then_inc(s_dnl, 1)

            def split_h(e, u):
                dve.wait_ge(s_esq, e + 1)
                if not (isinstance(e, int) and e < 2):
                    dve.wait_ge(s_yd, 2 * e - 2)
                dve.tensor_copy(hh[:, u % 2, :], hq[:, u % 2, :]).then_inc(s_ehh, 1)
                dve.wait_ge(s_ehh, e + 1)
                dve.tensor_tensor(hl[:, u % 2, :], hq[:, u % 2, :], hh[:, u % 2, :].bitcast(FP), ALU.subtract).then_inc(s_ehl, 1)

            def xt_low(e, i, u):
                dve.wait_ge(s_xg[u], (i + 1) * 32)
                if not (isinstance(e, int) and e < RAW):
                    dve.wait_ge(s_y, 2 * (e - RAW + 1))
                dve.tensor_copy(wx[:, u, :][:, :, None], xe[:, u, :, bass.ds(e + C, 1)]).then_inc(s_wx, 1)
                for n in range(2):
                    dve.wait_ge(s_thi, 2 * e + n + 1)
                    dve.tensor_tensor(xt[u % 2][1][:, 2 * n:2 * n + 2, :].rearrange("p c s -> p (c s)"), tbank[n][:, :],
                                      xt[u % 2][0][:, 2 * n:2 * n + 2, :].rearrange("p c s -> p (c s)").bitcast(FP),
                                      ALU.subtract).then_inc(s_tlo, 1)

            def step(e, i, u):
                if has(e, 1):
                    up_low(e + 1, (u + 1) % PER)
                if has(e, 0):
                    down_low(e, u)
                if has(e, 1):
                    xt_low(e + 1, i + (u + 1) // PER, (u + 1) % PER)
                if has(e, 0):
                    split_h(e, u)

            turns(dve, step)

        @block.gpsimd
        def _(pl):
            def wkv(n):
                pl.wait_ge(s_ek, n + 1)
                pl.tensor_tensor(ekv[n % 2], ek[n % 2], kt[n % 2], ALU.mult).then_inc(s_ekv, 1)
                pl.wait_ge(s_eu, n + 1)
                pl.tensor_tensor(eu[n % 2], eu[n % 2], ek[n % 2], ALU.subtract).then_inc(s_du, 1)
                pl.wait_ge(s_du, n + 1)
                pl.tensor_tensor(dv[n % 2], eu[n % 2], kt[n % 2], ALU.mult).then_inc(s_dv, 1)

            def flat_low(n):
                b, c = divmod(n, NC)
                pl.wait_ge(s_fhi, n + 1)
                pl.tensor_tensor(flat_lo[b % 2][:, c, :], fT[:, b % 2, c, :], flat_hi[b % 2][:, c, :].bitcast(FP),
                                 ALU.subtract).then_inc(s_flo, 1)

            def h_low(J):
                pl.wait_ge(s_hh, J + 1)
                pl.tensor_tensor(hl[:, J % 3, :], hq[:, J % 2, :], hh[:, J % 3, :].bitcast(FP), ALU.subtract).then_inc(s_hl, 1)

            def shared_weights_low(q):
                pl.wait_ge(s_swh, q + 1)
                pl.tensor_tensor(chunk((sup[1], sdn[1]), q), staging(q), chunk((sup[0], sdn[0]), q).bitcast(FP),
                                 ALU.subtract).then_inc(s_swl, 1)

            def add_x(t):
                pl.wait_ge(s_accf, t + 1)
                pl.wait_ge(s_xr[t % 2], 16 * (t // 2 + 1))
                pl.tensor_tensor(yb[:, t % 2, :], yb[:, t % 2, :], yb[:, 2 + t % 2, :], ALU.add).then_inc(s_yx, 1)

            def store_weights(b):
                pl.wait_ge(s_w, b + 1)
                pl.dma_start(rows[b * T:(b + 1) * T, C:C + E].rearrange("(i p) e -> p i e", p=P), wsel[:, :, :]).then_inc(s_wst, 16)

            n = [0]

            def seq(ins):
                n[0] += 1
                ins.then_inc(s_ix, 1)
                pl.wait_ge(s_ix, n[0])

            seq(pl.memset(ident[:, :], 0.0))
            seq(pl.affine_select(out=ident[:, :], in_=ident[:, :], compare_op=ALU.not_equal, fill=1.0, base=0,
                                 pattern=[[-1, P]], channel_multiplier=1))
            seq(pl.memset(ones[:, :], 1.0))
            seq(pl.affine_select(out=lower[:, :], in_=ones[:, :], compare_op=ALU.is_gt, fill=0.0, base=0,
                                 pattern=[[1, P]], channel_multiplier=-1))
            seq(pl.iota(iota[:, :], pattern=[[1, E]], base=0, channel_multiplier=0, allow_small_or_imprecise_dtypes=True))
            seq(pl.iota(tid[:, :], pattern=[[P, B * NI]], base=1, channel_multiplier=1, allow_small_or_imprecise_dtypes=True))
            seq(pl.iota(slot[:, :], pattern=[[P, NS]], base=NTOK + 1, channel_multiplier=1, allow_small_or_imprecise_dtypes=True))
            seq(pl.iota(iota16[:, :, :], pattern=[[1, SA], [0, EL]], base=0, channel_multiplier=0, allow_small_or_imprecise_dtypes=True))
            seq(pl.memset(blk[:, :], 0.0))
            for m in range(P // EL):
                seq(pl.affine_select(out=blk[:, :], in_=blk[:, :], compare_op=ALU.not_equal, fill=1.0, base=-EL * m,
                                     pattern=[[-1, EL]], channel_multiplier=1))
            seq(pl.tensor_copy(sel[:, :, :], blk[:, :, None].to_broadcast([P, EL, NS])))
            seq(pl.affine_select(out=sel[:, :, :], in_=sel[:, :, :], compare_op=ALU.is_ge, fill=0.0, base=0,
                                 pattern=[[0, EL], [-P // NS, NS]], channel_multiplier=1))
            seq(pl.affine_select(out=sel[:, :, :], in_=sel[:, :, :], compare_op=ALU.is_gt, fill=0.0, base=P // NS,
                                 pattern=[[0, EL], [P // NS, NS]], channel_multiplier=-1))
            seq(pl.memset(low8[:, :, :], 1.0))
            seq(pl.affine_select(out=low8[:, :, :], in_=low8[:, :, :], compare_op=ALU.is_ge, fill=0.0, base=0,
                                 pattern=[[-P // NS, NS], [-8, 8]], channel_multiplier=1))
            seq(pl.affine_select(out=low8[:, :, :], in_=low8[:, :, :], compare_op=ALU.is_gt, fill=0.0, base=8,
                                 pattern=[[P // NS, NS], [8, 8]], channel_multiplier=-1))
            seq(pl.tensor_tensor(low[:, :], low8[:, 0, :], low8[:, 1, :], ALU.add))
            pl.memset(hq[:, :, :], 0.0).then_inc(s_zero, 1)
            pl.sem_inc(s_cst, 1)
            base = n[0]
            wkv(0)
            for s in range(B + 1):
                for c in range(NC):
                    m = NC * s + c
                    if m + 1 < NT:
                        wkv(m + 1)
                    for q in SPLIT_AT.get(m, ()):
                        shared_weights_low(q)
                    if s >= 1 and c == 0:
                        flat_low(m - 1)
                    if 1 <= s < B:
                        h_low(NJ * (s - 1) + 2 * c)
                        h_low(NJ * (s - 1) + 2 * c + 1)
                    if c >= 1 and m < NT:
                        flat_low(m - 1)
                    if 1 <= s < B and c == 2:
                        store_weights(s - 1)
                if 1 <= s < B:
                    for i in range(NI):
                        add_x(NI * (s - 1) + i)

            def copy_index(dst, src, at, count):
                pl.tensor_copy(dst, src[:, bass.ds(at, NS)]).then_inc(s_ix, 1)
                pl.wait_ge(s_ix, count)

            def gather(e, i, u, count):
                if not (isinstance(e, int) and e < RAW):
                    pl.wait_ge(s_tr, 2 * (e - RAW) + 2)
                    pl.wait_ge(s_wx, e - RAW + 1)
                if not (isinstance(e, int) and e < 2):
                    pl.wait_ge(s_xg[(u - 2) % RAW], (i + (u - 2) // RAW + 1) * 32)
                copy_index(gi[:, u % 2, :], tgat, e * NS, count)
                pl.sem_inc(s_go, 1)
                for h in range(NS):
                    pl.indirect_dma_start(xe[:, u, h, :], None, rows[:, :],
                                          bass.IndirectOffsetOnAxis(ap=gi[:, u % 2, h:h + 1], axis=0)).then_inc(s_xg[u], 16)

            def add_result(e, i, u, count):
                if not (isinstance(e, int) and e < 1):
                    pl.wait_ge(s_sc[(u - 1) % 2], (2 * (i + (u - 1) // PER) + ((u - 1) % PER) // 2 + 1) * 32)
                copy_index(si[:, u % 2, :], tscat, e * NS, count)
                pl.wait_ge(s_y, 2 * e + 2)
                pl.sem_inc(s_go, 1)
                for h in range(NS):
                    pl.indirect_dma_start(out[:, :], bass.IndirectOffsetOnAxis(ap=si[:, u % 2, h:h + 1], axis=0),
                                          yb[:, 2 * (u % 2) + h, :], None, compute_op=ALU.add).then_inc(s_sc[u % 2], 16)

            for j in range(NJ):
                h_low(NJ * (B - 1) + j)
                if j == 4:
                    store_weights(B - 1)
                    pl.wait_ge(s_tab, 1)
                    pl.wait_ge(s_wst, 16 * B)
                    for x in (0, 1):
                        pl.wait_ge(s_rowd[x], 16 * NI * B // 2)
                    for e in range(2):
                        gather(e, 0, e, base + e + 1)
            for i in range(NI):
                add_x(NI * (B - 1) + i)
            for x in (0, 1):
                pl.wait_ge(s_out[x], 16 * NI * B // 2)
            pl.wait_ge(s_zst, 16)

            def step(e, i, u):
                if isinstance(e, int):
                    done = base + 2 + max(0, min(e, E - 3) + 1) + max(0, e - 1)
                else:
                    done = e * 2 + (base + 2)
                if has(e, 3):
                    gather(e + 3, i + (u + 3) // PER, (u + 3) % PER, done + 1)
                    done = done + 1
                if has(e, -1):
                    add_result(e - 1, i + (u - 1) // PER, (u - 1) % PER, done + 1)

            turns(pl, step)
            for x in (0, 1):
                pl.wait_ge(s_sc[x], 32 * E // 2)


def kernel(**inputs):
    import numpy as np
    import concourse.bacc as bacc
    from concourse.bass_utils import run_bass_kernel_spmd

    a = {k: np.asarray(v) for k, v in inputs.items()}
    x, side = a["x"], a["fside_BxSxS_0"]
    up, down = a["L0_ffn_up_w"], a["L0_ffn_down_w"]
    arrays = {
        "xT": np.transpose(x, (2, 0, 1)),
        "kT": np.transpose(side, (2, 0, 1)),
        "xrow": x.reshape(NTOK, C),
        "cond": a["cond_512"],
        "wdec": a["L0_cond_w"].reshape(NC, P).T,
        "ubon": a["L0_cond_u"].reshape(NC, P).T,
        "gateT": a["L0_ffn_gate_w"].T.reshape(NC, P, E).transpose(1, 0, 2),
        "bias": a["L0_ffn_bias_corr"],
        "upT": up.transpose(0, 2, 1).reshape(E, NC, P, H).transpose(0, 2, 1, 3).reshape(E, P, NC * H),
        "downT": down.transpose(0, 2, 1).reshape(E, NH, P, C).transpose(0, 2, 1, 3).reshape(E, P, NH * C),
        "supT": a["L0_ffn_shared_up_w"].T.reshape(NC, P, HS).transpose(1, 0, 2),
        "sdownT": a["L0_ffn_shared_down_w"].T.reshape(NJ, P, C).transpose(1, 0, 2),
    }
    nc = bacc.Bacc("TRN2", target_bir_lowering=False, num_devices=1)
    given, args = {}, []
    for name, value in arrays.items():
        given[name] = np.ascontiguousarray(value)
        args.append(nc.dram_tensor(name, given[name].shape, FP, kind="ExternalInput").ap())
    out = nc.dram_tensor("out_rows", [NTOK + CAP, C], FP, kind="ExternalOutput").ap()
    adaln_moe_kernel(nc, *args, out)
    got = run_bass_kernel_spmd(nc, [given], core_ids=[0]).results[0]["out_rows"]
    return got[:NTOK].reshape(B, T, C)
```

```python
from contextlib import ExitStack

import concourse.bass as bass
from concourse import mybir
from concourse.alu_op_type import AluOpType as ALU

FP = mybir.dt.float32
FR = mybir.dt.float32r
F16 = mybir.dt.float16
I32 = mybir.dt.int32
U32 = mybir.dt.uint32
ACT = mybir.ActivationFunctionType
AX = mybir.AxisListType

B, T, C = 4, 512, 512
NTOK = B * T
TD = 128
E, G, TKG, K, H = 32, 8, 4, 4, 256
EG = E // G
HS = 1024
CAP = 256
SCALE = 2.5
P = 128
NC = C // P
NI = T // P
NJ = HS // P
NH = H // P
NS = CAP // P
SA, SB = CAP // 16, 16
EL = P // SA
NG = E // EL
ROW = C + E
KLIM = 30.0
RAW = 4


def adaln_moe_kernel(nc, xT, kT, xrow, cond, wdec, ubon, gateT, bias, upT, downT, supT, sdownT, out):
    rows = nc.dram_tensor("token_rows", [NTOK, ROW], FP, kind="Internal").ap()

    ctx = ExitStack()
    with ctx:
        def sb(name, shape, dt=FP):
            return ctx.enter_context(nc.sbuf_tensor(name, shape, dt))

        def sem(name):
            return ctx.enter_context(nc.semaphore(name))

        work = sb("work", [P, 19, T])
        kt = [work[:, n, :] for n in (0, 1)]
        er = [work[:, n, :] for n in (2, 3, 18)]
        ek = [work[:, n, :] for n in (4, 5)]
        eu = [work[:, n, :] for n in (6, 7)]
        ekv = [work[:, n, :] for n in (8, 9)]
        dv = [work[:, n, :] for n in (10, 11)]
        num = [work[:, n, :] for n in (12, 13)]
        den = [work[:, n, :] for n in (14, 15)]
        nb, db = work[:, 16, :], work[:, 17, :]
        raw = work[:, 0:16, :].rearrange("p (s n) t -> p s (n t)", s=RAW)
        pool = sb("flat_or_gathered", [P, RAW * NS * ROW])
        fT = pool[:, 0:2 * NC * T].rearrange("p (b c t) -> p b c t", b=2, c=NC)
        xe = pool[:, :].rearrange("p (s h r) -> p s h r", s=RAW, h=NS)
        parts = [sb(f"parts{n}", [P, 2, NC * T], FR) for n in (0, 1)]
        flat_hi = [x[:, 0, :].rearrange("p (c t) -> p c t", c=NC) for x in parts]
        flat_lo = [x[:, 1, :].rearrange("p (c t) -> p c t", c=NC) for x in parts]
        UPW = NC * H
        DNW = NH * C
        sup = [sb(f"shared_up{n}", [P, NC, HS], FR) for n in (0, 1)]
        sdn = [sb(f"shared_down{n}", [P, NJ, C], FR) for n in (0, 1)]
        xt_even = [sb(f"xt{n}", [P, NC, CAP], FR) for n in (0, 1)]
        xt = [xt_even, [x[:, 0, :].rearrange("p (c s) -> p c s", c=NC) for x in sup]]
        hr = sb("h_relu", [P, T])
        hq = sb("h_square", [P, 2, T])
        hh = sb("h_hi", [P, 3, T], FR)
        hl = sb("h_lo", [P, 3, T], FR)
        yb = sb("y", [P, 4, C])
        rowb = sb("rows_out", [P, 2, C])
        gate = rowb[:, 1, 0:NC * E].rearrange("p (c e) -> p c e", c=NC)
        gate_hi = sb("gate_hi", [P, NC, E], FR)
        gate_lo = sb("gate_lo", [P, NC, E], FR)
        biasb = sb("bias_all", [P, E])
        dec = sb("decay", [P, B, NC])
        wcol = sb("w_col", [P, NC])
        ucol = sb("u_col", [P, NC])
        tf = sb("tf", [P, B])
        tfd = sb("tf_decay", [P, B])
        tfi = sb("tf_scale", [P, B])
        ident = sb("ident", [P, P])
        lower = sb("before", [P, P], F16)
        ones = sb("ones", [P, P], F16)
        iota = sb("iota", [P, E])
        tid = sb("token_id", [P, B * NI])
        blk = sb("blk_mask", [P, EL])
        msk = hr[:, 0:P].rearrange("p (e m) -> p e m", e=EL)
        low8 = sb("low_mask", [P, NS, 8])
        low = sb("low_sum", [P, 8])
        sel = sb("sel", [P, EL, NS], F16)
        slot = sb("dummy_row", [P, NS])
        ex = sb("r_exp", [P, NI, E])
        sc = sb("r_score", [P, NI, E])
        scb = sb("r_biased", [P, NI, E])
        pmx = sb("r_pair_max", [P, NI * G, 2])
        pmn = sb("r_pair_min", [P, NI * G, 2])
        gs = sb("r_group", [P, NI * G])
        g1 = sb("r_group1", [P, NI * G])
        g2 = sb("r_group2", [P, NI * G])
        top = sb("r_top", [P, NI, 8])
        tix = sb("r_top_index", [P, NI, 8], U32)
        geq = sb("r_group_eq", [P, NI, TKG, G])
        eeq = sb("r_expert_eq", [P, NI, K, E], F16)
        mcnt = sb("r_mask_count", [P, E])
        gmask = sb("r_group_mask", [P, NI, G])
        tix16 = sb("r_top_index16", [P, NI, K], F16)
        expert16 = sb("expert_number16", [P, E], F16)
        mask16 = sb("r_mask16", [P, NI, E], F16)
        msum = sb("r_mask_sum", [P, 2, E], F16)
        wsel = sb("r_weight", [P, NI, E])
        wsum = sb("r_weight_sum", [P, NI])
        pint = sb("r_slot", [P, NI, E], I32)
        pa = scb[:, :, :].bitcast(I32)
        pbt = sc[:, :, :].bitcast(I32)
        pa16 = sb("r_slot_a16", [P, NI, E], F16)
        pb16 = sb("r_slot_b16", [P, NI, E], F16)
        oa = sb("onehot_a", [P, NI, NG, SA * EL], F16)
        ob = sb("onehot_b", [P, NI, NG, SB * EL], F16)
        iota16 = sb("iota16", [P, SA, EL], F16)
        tval = db[:, 0:NS * E]
        tgat = sb("t_gather", [P, NS * E], I32)
        tscat = sb("t_scatter", [P, NS * E], I32)
        tzero = db[:, NS * E:2 * NS * E]
        blkbig = nb.rearrange("p (g b e) -> p g b e", g=NG, e=EL)
        dblk = db[:, 2 * NS * E:2 * NS * E + NG * SB].rearrange("p (g b) -> p g b", g=NG)
        lsel = oa[:, 0, :, :].rearrange("p g (a b) -> p g a b", a=8)
        gi = sb("gather_index", [P, 2, NS], I32)
        si = sb("scatter_index", [P, 2, NS], I32)
        wx = sb("slot_weight", [P, RAW, NS])

        bank = [ctx.enter_context(nc.psum_tensor(f"bank{n}", [P, T], FP)) for n in range(8)]
        acc, ring, misc, idxb = bank[0:4], bank[4:6], bank[6], bank[7]
        ybank, tbank = bank[0:2], bank[6:8]

        s_gate, s_gparts, s_cond, s_cst = sem("s_gate"), sem("s_gate_parts"), sem("s_cond"), sem("s_constants")
        s_wdec, s_ubon = sem("s_w_col"), sem("s_u_col")
        s_k = [sem("s_k0"), sem("s_k1")]
        s_r = [sem("s_r0"), sem("s_r1"), sem("s_r2")]
        s_stage = [sem(f"s_stage{n}") for n in range(4)]
        s_swh, s_swl = sem("s_shared_hi"), [sem("s_shared_lo_even"), sem("s_shared_lo_odd")]
        s_vec = sem("s_vector_chain")
        s_dexp, s_tfe, s_act = sem("s_decay_exp"), sem("s_tf_exp"), sem("s_scalar_chain")
        s_neg, s_dec = sem("s_tf_neg"), sem("s_decay")
        s_clamp, s_ek, s_eu, s_er = sem("s_clamped"), sem("s_ek"), sem("s_eu"), sem("s_er")
        s_ekv, s_du, s_dv = sem("s_ekv"), sem("s_du"), sem("s_dv")
        s_den, s_rcp = sem("s_den"), sem("s_reciprocal")
        s_flat, s_fhi, s_flo = sem("s_flat"), sem("s_flat_hi"), sem("s_flat_lo")
        s_full, s_free = sem("s_ring_full"), sem("s_ring_free")
        s_rowe, s_rowd = sem("s_row_copied"), [sem("s_row_stored0"), sem("s_row_stored1")]
        s_lg, s_lgx, s_lgt = sem("s_logits"), sem("s_logits_exp"), sem("s_logits_turned")
        s_mask, s_w, s_wst = sem("s_mask"), sem("s_weights"), sem("s_weights_stored")
        s_pos, s_pint, s_oh, s_ob, s_obt, s_idx = sem("s_pos"), sem("s_pos_read"), sem("s_onehot"), sem("s_onehot_b"), sem("s_onehot_b_numbered"), sem("s_idx")
        s_lsel, s_sel, s_tab = sem("s_lsel"), sem("s_sel"), sem("s_table")
        s_sq, s_hh, s_hl, s_dn = sem("s_square"), sem("s_h_hi"), sem("s_h_lo"), sem("s_down")
        s_acc, s_accf = sem("s_acc"), sem("s_acc_copied")
        s_xr = [sem(f"s_xrow{n}") for n in range(NI)]
        s_out = [sem(f"s_out{n}") for n in range(NI)]
        s_num, s_numdv, s_own = sem("s_num"), sem("s_num_plus_dv"), sem("s_num_times_y")
        s_zero, s_zst = sem("s_zero"), sem("s_zero_stored")
        s_raw = [sem(f"s_raw{n}") for n in range(RAW)]
        s_xg = [sem(f"s_gathered{n}") for n in range(RAW)]
        s_uph, s_upl, s_dnh, s_dnl = sem("s_up_hi"), sem("s_up_lo"), sem("s_down_hi"), sem("s_down_lo")
        s_tr, s_thi, s_tlo, s_wx = sem("s_transposed"), sem("s_xt_hi"), sem("s_xt_lo"), sem("s_slot_weight")
        s_esq, s_ehh, s_ehl = sem("s_e_square"), sem("s_e_hi"), sem("s_e_lo")
        s_yd, s_y = sem("s_y_done"), sem("s_y_scaled")
        s_sc = [sem("s_scattered0"), sem("s_scattered1")]
        s_ix = sem("s_index_copied")
        s_go = sem("s_pair_may_go")

        NT = B * NC
        NROW = NI + NJ
        NCH = 8
        CH = HS
        PER = RAW
        SPLIT_AT = {0: (0, 1), 1: (2,), 2: (3,), 3: (4,), 4: (5,), 5: (6,), 6: (7,)}
        SCALE_AT = (0, 1)
        LOAD_AT = {1: (4, 5), 4: (6,), 5: (7,)}

        def pool_scales(n):
            return n // NC >= 1 and n % NC in SCALE_AT

        def wait(eng, s, v):
            if not isinstance(v, int) or v > 0:
                eng.wait_ge(s, v)

        def chunk(parts_, q):
            up, dn = parts_
            return up[:, q, :] if q < NC else dn[:, 2 * (q - NC):2 * (q - NC) + 2, :].rearrange("p j c -> p (j c)")

        def staging(q):
            place_ = fT[:, 1, :, :] if q in (2, 3) else yb
            return place_[:, 2 * (q % 2):2 * (q % 2) + 2, :].rearrange("p a c -> p (a c)")

        def turns(eng, step):
            for e in range(-1, PER):
                step(e, e // PER, e % PER)
            with eng.Fori(1, E // PER - 1) as i:
                for u in range(PER):
                    step(i * PER + u, i, u)
            for e in range(E - PER, E + 1):
                step(e, e // PER, e % PER)

        def has(e, d):
            return not isinstance(e, int) or 0 <= e + d < E

        block = ctx.enter_context(nc.Block())

        @block.sync
        def _(sp):
            def load_tile(n):
                b, c = divmod(n, NC)
                if n >= 2:
                    sp.wait_ge(s_dv, n - 1)
                sp.dma_start(kt[n % 2], kT[c * P:(c + 1) * P, b, :]).then_inc(s_k[n % 2], 16)
                if n >= 3:
                    sp.wait_ge(s_flat, n - 2)
                sp.dma_start(er[n % 3], xT[c * P:(c + 1) * P, b, :]).then_inc(s_r[n % 3], 16)

            def load_stage(q):
                if q >= 4:
                    sp.wait_ge(s_swl[q % 2], 1 if q < 6 else 3)
                src = supT[:, q, :] if q < NC else sdownT[:, 2 * (q - NC):2 * (q - NC) + 2, :].rearrange("p j c -> p (j c)")
                sp.dma_start(staging(q), src).then_inc(s_stage[q % 4], 16)

            def rows_of_x(b):
                for i in range(NI):
                    if b == 0:
                        for x in (0, 1):
                            sp.wait_ge(s_swl[x], NCH // 2)
                    else:
                        sp.wait_ge(s_out[i], 16 * b)
                    sp.dma_start(yb[:, i, :], xrow[b * T + i * P:b * T + (i + 1) * P, :]).then_inc(s_xr[i], 16)

            def results_of(b):
                for i in range(NI):
                    sp.wait_ge(s_accf, NI * b + i + 1)
                    sp.dma_start(out[b * T + i * P:b * T + (i + 1) * P, :], yb[:, i, :]).then_inc(s_out[i], 16)

            sp.dma_start(rowb[:, 0, :], cond.rearrange("b t -> (b t)").partition_broadcast(P)).then_inc(s_cond, 16)
            sp.dma_start(kt[0], kT[0:P, 0, :]).then_inc(s_k[0], 16)
            sp.dma_start(wcol[:, :], wdec).then_inc(s_wdec, 16)
            sp.dma_start(ucol[:, :], ubon).then_inc(s_ubon, 16)
            sp.dma_start(er[0], xT[0:P, 0, :]).then_inc(s_r[0], 16)
            load_tile(1)
            for q in range(4):
                load_stage(q)
            for s in range(B + 1):
                for c in range(NC):
                    n = NC * s + c + 2
                    if n < NT:
                        load_tile(n)
                    if s >= 2 and c == 1:
                        results_of(s - 2)
                    for q in LOAD_AT.get(n - 2, ()):
                        load_stage(q)
                if s == 0:
                    sp.wait_ge(s_zero, 1)
                    sp.dma_start(out[NTOK:NTOK + CAP, :].rearrange("(h p) c -> p h c", h=NS),
                                 hq[:, :, :]).then_inc(s_zst, 16)
                if s >= 1:
                    rows_of_x(s - 1)
                    if s == B:
                        results_of(s - 1)
                if s == B - 1:
                    sp.wait_ge(s_flat, NT)
                    for x in (0, 1):
                        sp.wait_ge(s_rowd[x], 16 * NI * B // 2)
                    for e in range(RAW):
                        sp.dma_start(raw[:, e, 0:UPW], upT[e]).then_inc(s_raw[e], 16)
                        sp.dma_start(raw[:, e, UPW:UPW + DNW], downT[e]).then_inc(s_raw[e], 16)

            with sp.Fori(1, E // RAW) as i:
                for u in range(RAW):
                    sp.wait_ge(s_upl, i * RAW + (u - RAW + 1))
                    sp.dma_start(raw[:, u, 0:UPW], upT[bass.ds(i * RAW + u, 1)].rearrange("o p n -> (o p) n")).then_inc(s_raw[u], 16)
                    sp.wait_ge(s_dnl, i * RAW + (u - RAW + 1))
                    sp.dma_start(raw[:, u, UPW:UPW + DNW], downT[bass.ds(i * RAW + u, 1)].rearrange("o p n -> (o p) n")).then_inc(s_raw[u], 16)

        @block.tensor
        def _(pe):
            def three(dst, lhs, rhs, first, last):
                pe.matmul(dst, lhs[0], rhs[0], start=first, stop=False)
                pe.matmul(dst, lhs[0], rhs[1], start=False, stop=False)
                return pe.matmul(dst, lhs[1], rhs[0], start=False, stop=last)

            def turn_tile(b, i):
                m = NROW * b + i
                wait(pe, s_free, m - 1)
                for c in range(NC):
                    ins = pe.transpose(ring[m % 2][:, c * P:(c + 1) * P], fT[:, b % 2, c, i * P:(i + 1) * P], ident[:, :])
                ins.then_inc(s_full, 1)

            def turn_rows(b):
                pe.wait_ge(s_flat, NC * (b + 1))
                if b == 0:
                    pe.wait_ge(s_cst, 1)
                for i in (0, 1):
                    turn_tile(b, i)
                pe.wait_ge(s_flo, NC * (b + 1))
                if b == 0:
                    pe.wait_ge(s_gparts, 1)
                else:
                    pe.wait_ge(s_pint, b)
                for c in range(NC):
                    ins = three(misc[0:E, :], [gate_hi[:, c, :], gate_lo[:, c, :]],
                                [x[b % 2][:, c, :] for x in (flat_hi, flat_lo)], c == 0, c == NC - 1)
                ins.then_inc(s_lg, 1)
                for i in (2, 3):
                    turn_tile(b, i)

            def turn_logits(b):
                pe.wait_ge(s_lgx, b + 1)
                for i in range(NI):
                    ins = pe.transpose(misc[:, i * E:(i + 1) * E], rowb[0:E, 0, i * P:(i + 1) * P], ident[0:E, 0:E])
                ins.then_inc(s_lgt, 1)

            def up(b, j):
                m = NROW * b + NI + j
                if b == 0 and j == 0:
                    for x in (0, 1):
                        pe.wait_ge(s_swl[x], NC // 2)
                pe.wait_ge(s_free, m - 1)
                for c in range(NC):
                    ins = three(ring[m % 2][:, :], [w[:, c, j * P:(j + 1) * P] for w in sup],
                                [flat_hi[b % 2][:, c, :], flat_lo[b % 2][:, c, :]], c == 0, c == NC - 1)
                ins.then_inc(s_full, 1)

            def down(b, j):
                J = NJ * b + j
                pe.wait_ge(s_hl, J + 1)
                if b == 0 and j % 2 == 0:
                    q = NC + j // 2
                    pe.wait_ge(s_swl[q % 2], q // 2 + 1)
                for i in range(NI):
                    if j == 0:
                        wait(pe, s_accf, NI * (b - 1) + i + 1)
                    ins = three(acc[i][:, :], [h[:, J % 3, i * P:(i + 1) * P] for h in (hh, hl)],
                                [w[:, j, :] for w in sdn], j == 0, j == NJ - 1)
                    if j == NJ - 1:
                        ins.then_inc(s_acc, 1)
                if j < NJ - 1:
                    ins.then_inc(s_dn, 1)

            def positions(b):
                pe.wait_ge(s_mask, b + 1)
                for i in range(NI):
                    dst = misc[:, P + i * E:P + (i + 1) * E]
                    pe.matmul(dst, lower[:, :], mask16[:, i, :], start=True, stop=False)
                    for before in range(i):
                        pe.matmul(dst, ones[:, :], mask16[:, before, :], start=False, stop=False)
                    ins = pe.matmul(dst, ones[:, :], msum[:, b % 2, :], start=False, stop=True)
                ins.then_inc(s_pos, 1)

            def places(b):
                pe.wait_ge(s_oh, b + 1)
                if b < B - 2:
                    pe.wait_ge(s_obt, b + 1)
                for i in range(NI):
                    for g in range(NG):
                        first, last = b == 0 and i == 0 and g == 0, b == B - 1 and i == NI - 1
                        ins = pe.matmul(idxb[:, g * P:(g + 1) * P],
                                        oa[:, i, g, :], ob[:, i, g, :],
                                        start=first, stop=last and g == NG - 1, skip_group_check=True)
                ins.then_inc(s_idx, 1)

            def table():
                pe.wait_ge(s_lsel, 1)
                for g in range(NG):
                    ins = pe.matmul(misc[:, 2 * P + g * 2 * EL:2 * P + (g + 1) * 2 * EL],
                                    lsel[:, g, :, :].rearrange("p a b -> p (a b)"), sel[:, :, :].rearrange("p e h -> p (e h)"), start=True, stop=True)
                ins.then_inc(s_sel, 1)

            def turn_expert(e, i, u):
                pe.wait_ge(s_xg[u], (i + 1) * 32)
                if isinstance(e, int) and e == 0:
                    pe.wait_ge(s_tab, 1)
                for n in range(2):
                    wait(pe, s_thi, 2 * (e - 1) + n + 1)
                    wait(pe, s_tlo, 2 * (e - 1) + n + 1)
                    for c in (2 * n, 2 * n + 1):
                        for h in range(NS):
                            o = (c % 2) * CAP + h * P
                            ins = pe.transpose(tbank[n][:, o:o + P], xe[:, u, h, c * P:(c + 1) * P], ident[:, :])
                    ins.then_inc(s_tr, 1)

            def expert_weights(u, dn):
                if dn:
                    return [parts[u % 2][:, x, UPW:UPW + DNW].rearrange("p (h c) -> p h c", h=NH) for x in (0, 1)]
                return [parts[u % 2][:, x, 0:UPW].rearrange("p (c h) -> p c h", c=NC) for x in (0, 1)]

            def expert_up(e, u):
                pe.wait_ge(s_tlo, 2 * e + 2)
                pe.wait_ge(s_upl, e + 1)
                pe.wait_ge(s_free, NROW * B + e - 1)
                w = expert_weights(u, False)
                for hb in range(NH):
                    for c in range(NC):
                        ins = three(ring[u % 2][:, hb * CAP:(hb + 1) * CAP], [x[:, c, hb * P:(hb + 1) * P] for x in w],
                                    [x[:, c, :] for x in xt[u % 2]], c == 0, c == NC - 1)
                ins.then_inc(s_full, 1)

            def expert_down(e, u):
                pe.wait_ge(s_ehl, e + 1)
                pe.wait_ge(s_dnl, e + 1)
                w = expert_weights(u, True)
                for h in range(NS):
                    if isinstance(e, int) and e == 0:
                        pe.wait_ge(s_accf, NI * B)
                    wait(pe, s_y, 2 * (e - 1) + h + 1)
                    for hb in range(NH):
                        ins = three(ybank[h][:, :], [x[:, u % 2, hb * CAP + h * P:hb * CAP + (h + 1) * P] for x in (hh, hl)],
                                    [x[:, hb, :] for x in w], hb == 0, hb == NH - 1)
                    ins.then_inc(s_yd, 1)

            for b in range(B):
                turn_rows(b)
                up(b, 0)
                up(b, 1)
                turn_logits(b)
                for j in range(NJ):
                    if j + 2 < NJ:
                        up(b, j + 2)
                    down(b, j)
                    if b >= 1 and j == (2 if b < B - 1 else 0):
                        places(b - 1)
                    if b < B - 1 and j == 5:
                        positions(b)
                    if b == B - 1:
                        if j == 0:
                            positions(b)
                        if j == 1:
                            places(b)
                        if j == 2:
                            table()
                        if j == NJ - 2:
                            turn_expert(0, 0, 0)

            def step(e, i, u):
                if has(e, 1) and not (isinstance(e, int) and e < 0):
                    turn_expert(e + 1, i + (u + 1) // PER, (u + 1) % PER)
                if has(e, 0):
                    expert_up(e, u)
                if has(e, -1):
                    expert_down(e - 1, (u - 1) % PER)

            turns(pe, step)

        @block.scalar
        def _(act):
            chain = [0]

            def link(ins):
                chain[0] += 1
                ins.then_inc(s_act, 1)
                return chain[0]

            act.preload_act_table_set("natural_log_exp_and_others")
            act.dma_start(gate, gateT).then_inc(s_gate, 16)
            act.dma_start(biasb[:, :], bias.partition_broadcast(P)).then_inc(s_gate, 16)
            act.wait_ge(s_wdec, 16)
            act.wait_ge(s_act, link(act.activation(wcol[:, :], wcol[:, :], ACT.Exp)))
            act.activation(wcol[:, :], wcol[:, :], ACT.Exp, scale=-1.0).then_inc(s_dexp, 1)
            act.wait_ge(s_neg, 1)
            act.activation(tf[:, :], tf[:, :], ACT.Exp).then_inc(s_tfe, 1)

            def exps(n):
                act.wait_ge(s_clamp, 2 * n + 1)
                act.activation(ek[n % 2], ek[n % 2], ACT.Exp).then_inc(s_ek, 1)
                act.wait_ge(s_clamp, 2 * n + 2)
                act.activation(eu[n % 2], eu[n % 2], ACT.Exp).then_inc(s_eu, 1)
                act.wait_ge(s_r[n % 3], 16 * (n // 3 + 1))
                act.wait_ge(s_act, link(act.activation(er[n % 3], er[n % 3], ACT.Exp, scale=-1.0)))
                if n == 0:
                    act.wait_ge(s_dec, 1)
                b = n // NC
                act.activation(er[n % 3], er[n % 3], ACT.Identity, bias=tfi[:, b:b + 1], scale=tfi[:, b:b + 1]).then_inc(s_er, 1)

            def reciprocal(n):
                act.wait_ge(s_den, n + 1)
                act.wait_ge(s_act, link(act.activation(er[n % 3], den[n % 2], ACT.Ln)))
                act.activation(er[n % 3], er[n % 3], ACT.Exp, scale=-1.0).then_inc(s_rcp, 1)

            def flat_high(n):
                b, c = divmod(n, NC)
                act.wait_ge(s_flat, n + 1)
                if b >= 2:
                    act.wait_ge(s_full, NROW * (b - 1))
                act.activation(flat_hi[b % 2][:, c, :], fT[:, b % 2, c, :], ACT.Copy).then_inc(s_fhi, 1)

            def shared_weights_high(q):
                act.wait_ge(s_stage[q % 4], 16 * (q // 4 + 1))
                act.activation(chunk((sup[0], sdn[0]), q), staging(q), ACT.Copy).then_inc(s_swh, 1)

            def post(J):
                b, j = divmod(J, NJ)
                act.wait_ge(s_full, NROW * b + NI + j + 1)
                wait(act, s_sq, J)
                act.activation(hr[:, :], ring[j % 2][:, :], ACT.Relu).then_inc(s_free, 1)
                act.wait_ge(s_free, NROW * b + NI + j + 1)
                wait(act, s_hl, J - 1)
                if J == 0:
                    act.wait_ge(s_zst, 16)
                act.activation(hq[:, J % 2, :], hr[:, :], ACT.Square).then_inc(s_sq, 1)
                act.wait_ge(s_sq, J + 1)
                if J >= 3:
                    last = J - 3
                    if last % NJ == NJ - 1:
                        act.wait_ge(s_acc, NI * (last // NJ + 1))
                    else:
                        act.wait_ge(s_dn, last - last // NJ + 1)
                act.activation(hh[:, J % 3, :], hq[:, J % 2, :], ACT.Copy).then_inc(s_hh, 1)

            def number_onehots(b):
                act.wait_ge(s_ob, b + 1)
                for i in range(NI):
                    ins = act.activation(ob[:, i, :, :].rearrange("p g k -> p (g k)"), ob[:, i, :, :].rearrange("p g k -> p (g k)"),
                                         ACT.Copy, scale=tid[:, b * NI + i:b * NI + i + 1])
                ins.then_inc(s_obt, 1)

            def rows_out(b):
                for i in range(NI):
                    t = NI * b + i
                    act.wait_ge(s_full, NROW * b + i + 1)
                    if t >= 2:
                        act.wait_ge(s_rowd[t % 2], 16 * (t // 2))
                        if i == 0:
                            act.wait_ge(s_lgt, b)
                    elif t == 0:
                        act.wait_ge(s_neg, 1)
                    else:
                        act.wait_ge(s_gparts, 1)
                    act.activation(rowb[:, t % 2, :], ring[i % 2][:, :], ACT.Copy).then_inc(s_free, 1)
                    act.wait_ge(s_free, NROW * b + i + 1)
                    act.dma_start(rows[t * P:(t + 1) * P, 0:C], rowb[:, t % 2, :]).then_inc(s_rowd[t % 2], 16)
                act.wait_ge(s_lg, b + 1)
                act.wait_ge(s_rowd[0], 16 * (NI * (b + 1) // 2))
                act.activation(rowb[0:E, 0, :], misc[0:E, :], ACT.Exp, scale=-1.0).then_inc(s_lgx, 1)

            def up_high(e, i, u):
                act.wait_ge(s_raw[u], (i + 1) * 32)
                if isinstance(e, int) and e < 2:
                    act.wait_ge(s_full, NROW * (B - 1 + e))
                else:
                    act.wait_ge(s_full, NROW * B + e - 1)
                act.activation(parts[u % 2][:, 0, 0:UPW], raw[:, u, 0:UPW], ACT.Copy).then_inc(s_uph, 1)

            def down_high(e, u):
                if not (isinstance(e, int) and e < 2):
                    act.wait_ge(s_yd, 2 * e - 2)
                act.activation(parts[u % 2][:, 0, UPW:UPW + DNW], raw[:, u, UPW:UPW + DNW], ACT.Copy).then_inc(s_dnh, 1)

            def xt_high(e, u):
                for n in range(2):
                    act.wait_ge(s_tr, 2 * e + n + 1)
                    if not (isinstance(e, int) and e == 0):
                        act.wait_ge(s_full, NROW * B + e - 1)
                    act.activation(xt[u % 2][0][:, 2 * n:2 * n + 2, :].rearrange("p c s -> p (c s)"), tbank[n][:, :],
                                   ACT.Copy).then_inc(s_thi, 1)

            def expert_square(e, u):
                act.wait_ge(s_full, NROW * B + e + 1)
                if isinstance(e, int) and e == 0:
                    act.wait_ge(s_sq, NJ * B)
                else:
                    act.wait_ge(s_esq, e)
                act.activation(hr[:, :], ring[u % 2][:, :], ACT.Relu).then_inc(s_free, 1)
                act.wait_ge(s_free, NROW * B + e + 1)
                if isinstance(e, int) and e < 2:
                    act.wait_ge(s_hl, NJ * B)
                else:
                    act.wait_ge(s_ehl, e - 1)
                act.activation(hq[:, u % 2, :], hr[:, :], ACT.Square).then_inc(s_esq, 1)

            def results(e, i, u):
                act.wait_ge(s_wx, e + 1)
                if isinstance(e, int) and e < 2:
                    for x in range(NI):
                        act.wait_ge(s_out[x], 16 * B)
                else:
                    act.wait_ge(s_sc[u % 2], (2 * i + u // 2) * 32)
                for h in range(NS):
                    act.wait_ge(s_yd, 2 * e + h + 1)
                    act.activation(yb[:, 2 * (u % 2) + h, :], ybank[h][:, :], ACT.Copy,
                                   scale=wx[:, u, h:h + 1]).then_inc(s_y, 1)

            exps(0)
            for s in range(B + 1):
                for c in range(NC):
                    n = NC * s + c
                    if n + 1 < NT:
                        exps(n + 1)
                    for q in SPLIT_AT.get(n, ()):
                        shared_weights_high(q)
                    if s >= 1 and c == 0:
                        if n < NT:
                            reciprocal(n)
                        if s > 1:
                            flat_high(n - 1)
                        rows_out(s - 1)
                    if 2 <= s < B and c == 1:
                        number_onehots(s - 2)
                    if s >= 1:
                        post(NJ * (s - 1) + 2 * c)
                    if c >= 1 or s == 0:
                        if n < NT:
                            reciprocal(n)
                    if s >= 1:
                        post(NJ * (s - 1) + 2 * c + 1)
                    if s == B and c == 2:
                        up_high(0, 0, 0)
                    if c >= 1 and n < NT:
                        flat_high(n - 1)
                    if n == NC - 1:
                        flat_high(n)

            def step(e, i, u):
                if has(e, 1) and not (isinstance(e, int) and e < 0):
                    up_high(e + 1, i + (u + 1) // PER, (u + 1) % PER)
                if has(e, 0):
                    down_high(e, u)
                if has(e, 1):
                    xt_high(e + 1, (u + 1) % PER)
                if has(e, 0):
                    expert_square(e, u)
                if has(e, -1):
                    results(e - 1, i + (u - 1) // PER, (u - 1) % PER)

            turns(act, step)

        @block.vector
        def _(dve):
            chain = [0]

            def link(ins):
                chain[0] += 1
                ins.then_inc(s_vec, 1)
                return chain[0]

            def tt(o, a, b_, op):
                return link(dve.tensor_tensor(o, a, b_, op))

            def after(n):
                dve.wait_ge(s_vec, n)

            dve.wait_ge(s_cond, 16)
            after(link(dve.tensor_reduce(tf[:, :], rowb[:, 0, :].rearrange("p (b t) -> p b t", b=B), AX.X, ALU.add)))
            dve.tensor_scalar(tf[:, :], tf[:, :], -1.0, 80.0, ALU.mult, ALU.min).then_inc(s_neg, 1)

            def clamp(n):
                dve.wait_ge(s_k[n % 2], 16 * (n // 2 + 1))
                if n >= 2:
                    dve.wait_ge(s_dv, n - 1)
                dve.tensor_scalar(ek[n % 2], kt[n % 2], KLIM, None, ALU.min).then_inc(s_clamp, 1)
                if n == 0:
                    dve.wait_ge(s_ubon, 16)
                dve.tensor_scalar(eu[n % 2], kt[n % 2], ucol[:, n % NC:n % NC + 1], KLIM, ALU.add,
                                  ALU.min).then_inc(s_clamp, 1)

            clamp(0)
            dve.wait_ge(s_tfe, 1)
            after(link(dve.tensor_scalar(tf[:, :], tf[:, :], 1.0, None, ALU.add)))
            after(link(dve.reciprocal(tf[:, :], tf[:, :])))
            n0 = link(dve.tensor_scalar(tfi[:, :], tf[:, :], 0.2, 0.8, ALU.mult, ALU.add))
            n1 = link(dve.tensor_scalar(tfd[:, :], tf[:, :], 0.5, 0.5, ALU.mult, ALU.add))
            after(n0)
            dve.reciprocal(tfi[:, :], tfi[:, :]).then_inc(s_dec, 1)
            dve.wait_ge(s_dexp, 1)
            after(n1)
            for b in range(B):
                n0 = link(dve.tensor_scalar(dec[:, b, :], wcol[:, :], tfd[:, b:b + 1], None, ALU.mult))
            link(dve.memset(msum[:, 0, :], 0.0))
            after(n0)

            def gate_parts():
                dve.wait_ge(s_gate, 32)
                after(link(dve.tensor_copy(gate_hi[:, :, :], gate)))
                dve.tensor_tensor(gate_lo[:, :, :], gate, gate_hi[:, :, :].bitcast(FP), ALU.subtract).then_inc(s_gparts, 1)

            def wkv(n):
                b, c = divmod(n, NC)
                d = dec[:, b, c:c + 1].to_broadcast([P, T])
                e_, v_, nf, df = ek[n % 2], ekv[n % 2], num[n % 2], den[n % 2]
                if n + 1 < NT:
                    clamp(n + 1)
                if n >= 2:
                    dve.wait_ge(s_flat, n - 1)
                dve.wait_ge(s_ek, n + 1)
                link(dve.tensor_tensor_scan(df, d, e_, 0.0, ALU.mult, ALU.add))
                a2 = link(dve.tensor_tensor_scan(db[:, ::-1], d, e_[:, ::-1], 0.0, ALU.mult, ALU.add))
                after(a2)
                a3 = tt(df, df, db, ALU.add)
                dve.wait_ge(s_du, n + 1)
                after(a3)
                a4 = tt(df, df, eu[n % 2], ALU.add)
                dve.wait_ge(s_er, n + 1)
                after(a4)
                dve.scalar_tensor_tensor(out=df, in0=df, scalar=1e-8, in1=er[n % 3], op0=ALU.max, op1=ALU.mult).then_inc(s_den, 1)
                if n >= 1 and n != NC:
                    divide(n - 1)
                dve.wait_ge(s_ekv, n + 1)
                link(dve.tensor_tensor_scan(nf, d, v_, 0.0, ALU.mult, ALU.add))
                a5 = link(dve.tensor_tensor_scan(nb[:, ::-1], d, v_[:, ::-1], 0.0, ALU.mult, ALU.add))
                after(a5)
                dve.tensor_tensor(nf, nf, nb, ALU.add).then_inc(s_num, 1)
                if n == NC - 1:
                    divide(n)

            def shared_weights_low(q):
                dve.wait_ge(s_swh, q + 1)
                dve.tensor_tensor(chunk((sup[1], sdn[1]), q), staging(q), chunk((sup[0], sdn[0]), q).bitcast(FP),
                                  ALU.subtract).then_inc(s_swl[1], 1)

            def divide(n):
                b, c = divmod(n, NC)
                dve.wait_ge(s_rcp, n + 1)
                a1 = tt(den[n % 2], den[n % 2], er[n % 3], ALU.mult)
                if b >= 2:
                    dve.wait_ge(s_flo, NC * (b - 1))
                    dve.wait_ge(s_lg, b - 1)
                if n in (NC, NC + 2):
                    dve.wait_ge(s_swl[(n - NC) // 2], 2)
                if pool_scales(n):
                    dve.wait_ge(s_own, n + 1)
                else:
                    dve.wait_ge(s_numdv, n + 1)
                    dve.tensor_tensor(num[n % 2], num[n % 2], er[n % 3], ALU.mult).then_inc(s_own, 1)
                    dve.wait_ge(s_own, n + 1)
                after(a1)
                dve.scalar_tensor_tensor(out=fT[:, b % 2, c, :], in0=den[n % 2], scalar=2.0, in1=num[n % 2],
                                         op0=ALU.subtract, op1=ALU.mult, reverse0=True).then_inc(s_flat, 1)

            def sums_out(b):
                for i in range(NI):
                    t = NI * b + i
                    dve.wait_ge(s_xr[i], 16 * (b + 1))
                    dve.wait_ge(s_acc, t + 1)
                    dve.tensor_tensor(yb[:, i, :], acc[i][:, :], yb[:, i, :], ALU.add).then_inc(s_accf, 1)

            def choose(b):
                dve.wait_ge(s_lgt, b + 1)
                if b == 0:
                    dve.wait_ge(s_gate, 32)
                    dve.wait_ge(s_cst, 1)
                if b >= 1:
                    dve.wait_ge(s_wst, 16 * b)
                    dve.wait_ge(s_pos, b)
                flat = lambda x: x[:, :, :].rearrange("p i e -> p (i e)")
                after(link(dve.tensor_scalar(flat(ex), misc[:, 0:NI * E], 1.0, None, ALU.add)))
                after(link(dve.reciprocal(flat(sc), flat(ex))))
                after(tt(scb[:, :, :], sc[:, :, :], biasb[:, None, :].to_broadcast([P, NI, E]), ALU.add))
                pair = flat(scb).rearrange("p (g q x) -> p g q x", q=2, x=2)
                tt(pmx[:, :, :], pair[:, :, :, 0], pair[:, :, :, 1], ALU.max)
                after(tt(pmn[:, :, :], pair[:, :, :, 0], pair[:, :, :, 1], ALU.min))
                tt(g1[:, :], pmx[:, :, 0], pmx[:, :, 1], ALU.min)
                tt(g2[:, :], pmn[:, :, 0], pmn[:, :, 1], ALU.max)
                after(tt(gs[:, :], pmx[:, :, 0], pmx[:, :, 1], ALU.max))
                after(tt(g1[:, :], g1[:, :], g2[:, :], ALU.max))
                after(tt(gs[:, :], gs[:, :], g1[:, :], ALU.add))
                for i in range(NI):
                    last = link(dve.max(top[:, i, :], gs[:, i * G:(i + 1) * G]))
                after(last)
                for i in range(NI):
                    last = link(dve.max_index(tix[:, i, :], top[:, i, :], gs[:, i * G:(i + 1) * G]))
                after(last)
                after(tt(geq[:, :, :, :], tix[:, :, 0:TKG][:, :, :, None].to_broadcast([P, NI, TKG, G]),
                         iota[:, 0:G][:, None, None, :].to_broadcast([P, NI, TKG, G]), ALU.is_equal))
                after(link(dve.tensor_reduce(gmask[:, :, :], geq[:, :, :, :].rearrange("p i k g -> p i g k"), AX.X, ALU.add)))
                after(tt(ex[:, :, :].rearrange("p i (g x) -> p (i g) x", x=EG), scb[:, :, :].rearrange("p i (g x) -> p (i g) x", x=EG),
                         gmask[:, :, :].rearrange("p i g -> p (i g)")[:, :, None].to_broadcast([P, NI * G, EG]), ALU.mult))
                for i in range(NI):
                    last = link(dve.max(top[:, i, :], ex[:, i, :]))
                after(last)
                for i in range(NI):
                    last = link(dve.max_index(tix[:, i, :], top[:, i, :], ex[:, i, :]))
                after(last)
                after(link(dve.tensor_copy(tix16[:, :, :], tix[:, :, 0:K])))
                after(tt(eeq[:, :, :, :], tix16[:, :, :][:, :, :, None].to_broadcast([P, NI, K, E]),
                         expert16[:, :][:, None, None, :].to_broadcast([P, NI, K, E]), ALU.is_equal))
                after(tt(eeq[:, :, 0:2, :], eeq[:, :, 0:2, :], eeq[:, :, 2:4, :], ALU.add))
                dve.tensor_tensor(mask16[:, :, :], eeq[:, :, 0, :], eeq[:, :, 1, :], ALU.add).then_inc(s_mask, 1)
                dve.wait_ge(s_mask, b + 1)
                last = tt(wsel[:, :, :], sc[:, :, :], mask16[:, :, :], ALU.mult)
                after(last)
                after(link(dve.tensor_reduce(wsum[:, :], wsel[:, :, :], AX.X, ALU.add)))
                if b < B - 1:
                    link(dve.tensor_reduce(mcnt[:, :], mask16[:, :, :].rearrange("p i e -> p e i"), AX.X, ALU.add))
                after(link(dve.tensor_scalar(wsum[:, :], wsum[:, :], 1e-20, None, ALU.add)))
                after(link(dve.reciprocal(wsum[:, :], wsum[:, :])))
                if b < B - 1:
                    tt(msum[:, (b + 1) % 2, :], msum[:, b % 2, :], mcnt[:, :], ALU.add)
                after(tt(wsel[:, :, :], wsel[:, :, :], wsum[:, :, None].to_broadcast([P, NI, E]), ALU.mult))
                dve.tensor_scalar(wsel[:, :, :], wsel[:, :, :], SCALE, None, ALU.mult).then_inc(s_w, 1)

            def place(b):
                dve.wait_ge(s_pos, b + 1)
                if b >= 1:
                    dve.wait_ge(s_idx, b)
                pos = misc[:, P:P + NI * E].rearrange("p (i e) -> p i e", i=NI)
                dve.scalar_tensor_tensor(out=ex[:, :, :], in0=pos, scalar=1.0, in1=mask16[:, :, :],
                                         op0=ALU.add, op1=ALU.mult).then_inc(s_pint, 1)
                dve.wait_ge(s_pint, b + 1)
                after(link(dve.tensor_scalar(pint[:, :, :], ex[:, :, :], 1.0, None, ALU.subtract)))
                link(dve.tensor_scalar(pa, pint[:, :, :], 4, None, ALU.arith_shift_right))
                after(link(dve.tensor_scalar(pbt, pint[:, :, :], SB - 1, None, ALU.bitwise_and)))
                link(dve.tensor_copy(pa16[:, :, :], pa))
                after(link(dve.tensor_copy(pb16[:, :, :], pbt)))
                def onehot(o, v, count):
                    return dve.tensor_tensor(
                        o[:, :, :, :].rearrange("p i g (a e) -> p (i g) a e", a=count),
                        v[:, :, :].rearrange("p i (g e) -> p (i g) e", g=NG)[:, :, None, :].to_broadcast([P, NI * NG, count, EL]),
                        iota16[:, None, :, :].to_broadcast([P, NI * NG, count, EL]), ALU.is_equal)

                onehot(ob, pb16, SB).then_inc(s_ob, 1)
                if b >= B - 2:
                    a0 = link(onehot(oa, pa16, SA))
                    dve.wait_ge(s_ob, b + 1)
                    for i in range(NI):
                        last = link(dve.tensor_scalar(ob[:, i, :, :], ob[:, i, :, :], tid[:, b * NI + i:b * NI + i + 1], None, ALU.mult))
                    after(last)
                    dve.sem_inc(s_oh, 1)
                else:
                    onehot(oa, pa16, SA).then_inc(s_oh, 1)

            def make_table():
                dve.wait_ge(s_idx, B)
                after(tt(blkbig, idxb[:, :].rearrange("p (g b e) -> p g b e", g=NG, e=EL),
                         blk[:, None, None, :].to_broadcast([P, NG, SB, EL]), ALU.mult))
                after(link(dve.tensor_reduce(dblk, blkbig, AX.X, ALU.add)))
                dve.tensor_tensor(lsel, dblk[:, :, None, :].to_broadcast([P, NG, 8, SB]),
                                  low[:, None, :, None].to_broadcast([P, NG, 8, SB]), ALU.mult).then_inc(s_lsel, 1)
                dve.wait_ge(s_sel, 1)
                after(link(dve.tensor_copy(tval, misc[:, 2 * P:2 * P + NS * E])))
                after(link(dve.tensor_scalar(tzero, tval, 0.0, None, ALU.is_equal)))
                link(dve.tensor_scalar(tgat[:, :], tval, 1.0, 0.0, ALU.subtract, ALU.max))
                after(tt(tzero.rearrange("p (e h) -> p e h", h=NS), tzero.rearrange("p (e h) -> p e h", h=NS),
                         slot[:, None, :].to_broadcast([P, E, NS]), ALU.mult))
                dve.scalar_tensor_tensor(out=tscat[:, :], in0=tval, scalar=-1.0, in1=tzero,
                                         op0=ALU.add, op1=ALU.add).then_inc(s_tab, 1)

            for s in range(B):
                for c in range(NC):
                    wkv(NC * s + c)
                    if s == 0 and c == 0:
                        gate_parts()
                    for q in SPLIT_AT.get(NC * s + c, ()):
                        if q % 2 == 1:
                            shared_weights_low(q)
                    if s >= 2 and c == 0:
                        place(s - 2)
                        sums_out(s - 2)
                    if s >= 1 and c == 1:
                        choose(s - 1)
            divide(NT - 1)
            place(B - 2)
            sums_out(B - 2)
            choose(B - 1)
            place(B - 1)
            make_table()

            def up_low(e, u):
                dve.wait_ge(s_uph, e + 1)
                dve.tensor_tensor(parts[u % 2][:, 1, 0:UPW], raw[:, u, 0:UPW],
                                  parts[u % 2][:, 0, 0:UPW].bitcast(FP), ALU.subtract).then_inc(s_upl, 1)

            def down_low(e, u):
                dve.wait_ge(s_dnh, e + 1)
                dve.tensor_tensor(parts[u % 2][:, 1, UPW:UPW + DNW], raw[:, u, UPW:UPW + DNW],
                                  parts[u % 2][:, 0, UPW:UPW + DNW].bitcast(FP), ALU.subtract).then_inc(s_dnl, 1)

            def split_h(e, u):
                dve.wait_ge(s_esq, e + 1)
                if not (isinstance(e, int) and e < 2):
                    dve.wait_ge(s_yd, 2 * e - 2)
                dve.tensor_copy(hh[:, u % 2, :], hq[:, u % 2, :]).then_inc(s_ehh, 1)
                dve.wait_ge(s_ehh, e + 1)
                dve.tensor_tensor(hl[:, u % 2, :], hq[:, u % 2, :], hh[:, u % 2, :].bitcast(FP), ALU.subtract).then_inc(s_ehl, 1)

            def xt_low(e, i, u):
                dve.wait_ge(s_xg[u], (i + 1) * 32)
                if not (isinstance(e, int) and e < RAW):
                    dve.wait_ge(s_y, 2 * (e - RAW + 1))
                dve.tensor_copy(wx[:, u, :][:, :, None], xe[:, u, :, bass.ds(e + C, 1)]).then_inc(s_wx, 1)
                for n in range(2):
                    dve.wait_ge(s_thi, 2 * e + n + 1)
                    dve.tensor_tensor(xt[u % 2][1][:, 2 * n:2 * n + 2, :].rearrange("p c s -> p (c s)"), tbank[n][:, :],
                                      xt[u % 2][0][:, 2 * n:2 * n + 2, :].rearrange("p c s -> p (c s)").bitcast(FP),
                                      ALU.subtract).then_inc(s_tlo, 1)

            def step(e, i, u):
                if has(e, 1):
                    up_low(e + 1, (u + 1) % PER)
                if has(e, 0):
                    down_low(e, u)
                if has(e, 1):
                    xt_low(e + 1, i + (u + 1) // PER, (u + 1) % PER)
                if has(e, 0):
                    split_h(e, u)
                if isinstance(e, int) and e == -1:
                    sums_out(B - 1)

            turns(dve, step)

        @block.gpsimd
        def _(pl):
            def wkv(n):
                pl.wait_ge(s_ek, n + 1)
                pl.tensor_tensor(ekv[n % 2], ek[n % 2], kt[n % 2], ALU.mult).then_inc(s_ekv, 1)
                if n > NC + 1 and n % NC == 1:
                    flat_low(n - 2)
                pl.wait_ge(s_eu, n + 1)
                pl.tensor_tensor(eu[n % 2], eu[n % 2], ek[n % 2], ALU.subtract).then_inc(s_du, 1)
                pl.wait_ge(s_du, n + 1)
                pl.tensor_tensor(dv[n % 2], eu[n % 2], kt[n % 2], ALU.mult).then_inc(s_dv, 1)

            def add_own(n):
                pl.wait_ge(s_num, n + 1)
                pl.tensor_tensor(num[n % 2], num[n % 2], dv[n % 2], ALU.add).then_inc(s_numdv, 1)
                if pool_scales(n):
                    pl.wait_ge(s_rcp, n + 1)
                    pl.wait_ge(s_numdv, n + 1)
                    pl.wait_ge(s_own, n)
                    pl.tensor_tensor(num[n % 2], num[n % 2], er[n % 3], ALU.mult).then_inc(s_own, 1)

            def flat_low(n):
                b, c = divmod(n, NC)
                pl.wait_ge(s_fhi, n + 1)
                pl.tensor_tensor(flat_lo[b % 2][:, c, :], fT[:, b % 2, c, :], flat_hi[b % 2][:, c, :].bitcast(FP),
                                 ALU.subtract).then_inc(s_flo, 1)

            def h_low(J):
                pl.wait_ge(s_hh, J + 1)
                pl.tensor_tensor(hl[:, J % 3, :], hq[:, J % 2, :], hh[:, J % 3, :].bitcast(FP), ALU.subtract).then_inc(s_hl, 1)

            def shared_weights_low(q):
                pl.wait_ge(s_swh, q + 1)
                pl.tensor_tensor(chunk((sup[1], sdn[1]), q), staging(q), chunk((sup[0], sdn[0]), q).bitcast(FP),
                                 ALU.subtract).then_inc(s_swl[0], 1)

            def store_weights(b):
                pl.wait_ge(s_w, b + 1)
                pl.dma_start(rows[b * T:(b + 1) * T, C:C + E].rearrange("(i p) e -> p i e", p=P), wsel[:, :, :]).then_inc(s_wst, 16)

            n = [0]

            def seq(ins):
                n[0] += 1
                ins.then_inc(s_ix, 1)
                pl.wait_ge(s_ix, n[0])

            seq(pl.memset(ident[:, :], 0.0))
            seq(pl.affine_select(out=ident[:, :], in_=ident[:, :], compare_op=ALU.not_equal, fill=1.0, base=0,
                                 pattern=[[-1, P]], channel_multiplier=1))
            seq(pl.memset(ones[:, :], 1.0))
            seq(pl.affine_select(out=lower[:, :], in_=ones[:, :], compare_op=ALU.is_gt, fill=0.0, base=0,
                                 pattern=[[1, P]], channel_multiplier=-1))
            seq(pl.iota(iota[:, :], pattern=[[1, E]], base=0, channel_multiplier=0, allow_small_or_imprecise_dtypes=True))
            seq(pl.iota(expert16[:, :], pattern=[[1, E]], base=0, channel_multiplier=0, allow_small_or_imprecise_dtypes=True))
            seq(pl.iota(tid[:, :], pattern=[[P, B * NI]], base=1, channel_multiplier=1, allow_small_or_imprecise_dtypes=True))
            seq(pl.iota(slot[:, :], pattern=[[P, NS]], base=NTOK + 1, channel_multiplier=1, allow_small_or_imprecise_dtypes=True))
            seq(pl.iota(iota16[:, :, :], pattern=[[1, SA], [0, EL]], base=0, channel_multiplier=0, allow_small_or_imprecise_dtypes=True))
            seq(pl.memset(msk[:, :, :], 0.0))
            seq(pl.affine_select(out=msk[:, :, :], in_=msk[:, :, :], compare_op=ALU.not_equal, fill=1.0, base=0,
                                 pattern=[[-1, EL], [-EL, P // EL]], channel_multiplier=1))
            for half in (8, 4, 2):
                seq(pl.tensor_tensor(msk[:, :, 0:half], msk[:, :, 0:half], msk[:, :, half:2 * half], ALU.add))
            seq(pl.tensor_tensor(blk[:, :, None], msk[:, :, 0:1], msk[:, :, 1:2], ALU.add))
            seq(pl.tensor_copy(sel[:, :, :], blk[:, :, None].to_broadcast([P, EL, NS])))
            seq(pl.affine_select(out=sel[:, :, :], in_=sel[:, :, :], compare_op=ALU.is_ge, fill=0.0, base=0,
                                 pattern=[[0, EL], [-P // NS, NS]], channel_multiplier=1))
            seq(pl.affine_select(out=sel[:, :, :], in_=sel[:, :, :], compare_op=ALU.is_gt, fill=0.0, base=P // NS,
                                 pattern=[[0, EL], [P // NS, NS]], channel_multiplier=-1))
            seq(pl.memset(low8[:, :, :], 1.0))
            seq(pl.affine_select(out=low8[:, :, :], in_=low8[:, :, :], compare_op=ALU.is_ge, fill=0.0, base=0,
                                 pattern=[[-P // NS, NS], [-8, 8]], channel_multiplier=1))
            seq(pl.affine_select(out=low8[:, :, :], in_=low8[:, :, :], compare_op=ALU.is_gt, fill=0.0, base=8,
                                 pattern=[[P // NS, NS], [8, 8]], channel_multiplier=-1))
            seq(pl.tensor_tensor(low[:, :], low8[:, 0, :], low8[:, 1, :], ALU.add))
            pl.sem_inc(s_cst, 1)
            base = n[0]
            wkv(0)
            wkv(1)
            pl.memset(hq[:, :, :], 0.0).then_inc(s_zero, 1)
            for s in range(B + 1):
                for c in range(NC):
                    m = NC * s + c
                    if 1 <= m < NT - 1:
                        wkv(m + 1)
                    if s >= 1 and c == 0:
                        if s == B:
                            flat_low(m - 1)
                        if m < NT:
                            add_own(m)
                    if 1 <= s < B:
                        h_low(NJ * (s - 1) + 2 * c)
                    if m < NT and (s == 0 or c >= 1):
                        add_own(m)
                    if 1 <= s < B:
                        h_low(NJ * (s - 1) + 2 * c + 1)
                    if c >= 1 and m < NT:
                        flat_low(m - 1)
                    if m == NC - 1:
                        flat_low(m)
                    for q in SPLIT_AT.get(m, ()):
                        if q % 2 == 0:
                            shared_weights_low(q)
                    if 1 <= s < B and c == 2:
                        store_weights(s - 1)

            def copy_index(dst, src, at, count):
                pl.tensor_copy(dst, src[:, bass.ds(at, NS)]).then_inc(s_ix, 1)
                pl.wait_ge(s_ix, count)

            def gather(e, i, u, count):
                if not (isinstance(e, int) and e < RAW):
                    pl.wait_ge(s_tr, 2 * (e - RAW) + 2)
                    pl.wait_ge(s_wx, e - RAW + 1)
                if not (isinstance(e, int) and e < 2):
                    pl.wait_ge(s_xg[(u - 2) % RAW], (i + (u - 2) // RAW + 1) * 32)
                copy_index(gi[:, u % 2, :], tgat, e * NS, count)
                pl.sem_inc(s_go, 1)
                for h in range(NS):
                    pl.indirect_dma_start(xe[:, u, h, :], None, rows[:, :],
                                          bass.IndirectOffsetOnAxis(ap=gi[:, u % 2, h:h + 1], axis=0)).then_inc(s_xg[u], 16)

            def add_result(e, i, u, count):
                if not (isinstance(e, int) and e < 1):
                    pl.wait_ge(s_sc[(u - 1) % 2], (2 * (i + (u - 1) // PER) + ((u - 1) % PER) // 2 + 1) * 32)
                copy_index(si[:, u % 2, :], tscat, e * NS, count)
                for h in range(NS):
                    pl.wait_ge(s_y, 2 * e + h + 1)
                    pl.sem_inc(s_go, 1)
                    pl.indirect_dma_start(out[:, :], bass.IndirectOffsetOnAxis(ap=si[:, u % 2, h:h + 1], axis=0),
                                          yb[:, 2 * (u % 2) + h, :], None, compute_op=ALU.add).then_inc(s_sc[u % 2], 16)

            for j in range(NJ):
                h_low(NJ * (B - 1) + j)
                if j == 4:
                    store_weights(B - 1)
                    pl.wait_ge(s_tab, 1)
                    pl.wait_ge(s_wst, 16 * B)
                    for x in (0, 1):
                        pl.wait_ge(s_rowd[x], 16 * NI * B // 2)
                    for e in range(RAW - 1):
                        gather(e, 0, e, base + e + 1)
            for i in range(NI):
                pl.wait_ge(s_out[i], 16 * B)
            pl.wait_ge(s_zst, 16)

            def step(e, i, u):
                if isinstance(e, int):
                    done = base + RAW - 1 + max(0, min(e, E - 3)) + max(0, e - 1)
                else:
                    done = e * 2 + (base + 2)
                if has(e, 3) and not (isinstance(e, int) and e < 0):
                    gather(e + 3, i + (u + 3) // PER, (u + 3) % PER, done + 1)
                    done = done + 1
                if has(e, -1):
                    add_result(e - 1, i + (u - 1) // PER, (u - 1) % PER, done + 1)

            turns(pl, step)
            for x in (0, 1):
                pl.wait_ge(s_sc[x], 32 * E // 2)


def kernel(**inputs):
    import numpy as np
    import concourse.bacc as bacc
    from concourse.bass_utils import run_bass_kernel_spmd

    a = {k: np.asarray(v) for k, v in inputs.items()}
    x, side = a["x"], a["fside_BxSxS_0"]
    up, down = a["L0_ffn_up_w"], a["L0_ffn_down_w"]
    arrays = {
        "xT": np.transpose(x, (2, 0, 1)),
        "kT": np.transpose(side, (2, 0, 1)),
        "xrow": x.reshape(NTOK, C),
        "cond": a["cond_512"],
        "wdec": a["L0_cond_w"].reshape(NC, P).T,
        "ubon": a["L0_cond_u"].reshape(NC, P).T,
        "gateT": a["L0_ffn_gate_w"].T.reshape(NC, P, E).transpose(1, 0, 2),
        "bias": a["L0_ffn_bias_corr"],
        "upT": up.transpose(0, 2, 1).reshape(E, NC, P, H).transpose(0, 2, 1, 3).reshape(E, P, NC * H),
        "downT": down.transpose(0, 2, 1).reshape(E, NH, P, C).transpose(0, 2, 1, 3).reshape(E, P, NH * C),
        "supT": a["L0_ffn_shared_up_w"].T.reshape(NC, P, HS).transpose(1, 0, 2),
        "sdownT": a["L0_ffn_shared_down_w"].T.reshape(NJ, P, C).transpose(1, 0, 2),
    }
    nc = bacc.Bacc("TRN2", target_bir_lowering=False, num_devices=1)
    given, args = {}, []
    for name, value in arrays.items():
        given[name] = np.ascontiguousarray(value)
        args.append(nc.dram_tensor(name, given[name].shape, FP, kind="ExternalInput").ap())
    out = nc.dram_tensor("out_rows", [NTOK + CAP, C], FP, kind="ExternalOutput").ap()
    adaln_moe_kernel(nc, *args, out)
    got = run_bass_kernel_spmd(nc, [given], core_ids=[0]).results[0]["out_rows"]
    return got[:NTOK].reshape(B, T, C)
```

```python
from contextlib import ExitStack

import concourse.bass as bass
from concourse import mybir
from concourse.alu_op_type import AluOpType as ALU

FP = mybir.dt.float32
FR = mybir.dt.float32r
F16 = mybir.dt.float16
I32 = mybir.dt.int32
U32 = mybir.dt.uint32
ACT = mybir.ActivationFunctionType
AX = mybir.AxisListType

B, T, C = 4, 512, 512
NTOK = B * T
TD = 128
E, G, TKG, K, H = 32, 8, 4, 4, 256
EG = E // G
HS = 1024
CAP = 256
SCALE = 2.5
P = 128
NC = C // P
NI = T // P
NJ = HS // P
NH = H // P
NS = CAP // P
SA, SB = CAP // 16, 16
EL = P // SA
NG = E // EL
ROW = C + E
KLIM = 30.0
RAW = 4


def adaln_moe_kernel(nc, xT, kT, xrow, cond, wdec, ubon, gateT, bias, upT, downT, supT, sdownT, out):
    rows = nc.dram_tensor("token_rows", [NTOK, ROW], FP, kind="Internal").ap()

    ctx = ExitStack()
    with ctx:
        def sb(name, shape, dt=FP):
            return ctx.enter_context(nc.sbuf_tensor(name, shape, dt))

        def sem(name):
            return ctx.enter_context(nc.semaphore(name))

        work = sb("work", [P, 19, T])
        kt = [work[:, n, :] for n in (0, 1)]
        er = [work[:, n, :] for n in (2, 3, 18)]
        ek = [work[:, n, :] for n in (4, 5)]
        eu = [work[:, n, :] for n in (6, 7)]
        ekv = [work[:, n, :] for n in (8, 9)]
        dv = [work[:, n, :] for n in (10, 11)]
        num = [work[:, n, :] for n in (12, 13)]
        den = [work[:, n, :] for n in (14, 15)]
        nb, db = work[:, 16, :], work[:, 17, :]
        raw = work[:, 0:16, :].rearrange("p (s n) t -> p s (n t)", s=RAW)
        pool = sb("flat_or_gathered", [P, RAW * NS * ROW])
        fT = pool[:, 0:2 * NC * T].rearrange("p (b c t) -> p b c t", b=2, c=NC)
        xe = pool[:, :].rearrange("p (s h r) -> p s h r", s=RAW, h=NS)
        parts = [sb(f"parts{n}", [P, 2, NC * T], FR) for n in (0, 1)]
        flat_hi = [x[:, 0, :].rearrange("p (c t) -> p c t", c=NC) for x in parts]
        flat_lo = [x[:, 1, :].rearrange("p (c t) -> p c t", c=NC) for x in parts]
        UPW = NC * H
        DNW = NH * C
        sup = [sb(f"shared_up{n}", [P, NC, HS], FR) for n in (0, 1)]
        sdn = [sb(f"shared_down{n}", [P, NJ, C], FR) for n in (0, 1)]
        xt_even = [sb(f"xt{n}", [P, NC, CAP], FR) for n in (0, 1)]
        xt = [xt_even, [x[:, 0, :].rearrange("p (c s) -> p c s", c=NC) for x in sup]]
        hr = sb("h_relu", [P, T])
        hq = sb("h_square", [P, 2, T])
        hh = sb("h_hi", [P, 3, T], FR)
        hl = sb("h_lo", [P, 3, T], FR)
        yb = sb("y", [P, 4, C])
        rowb = sb("rows_out", [P, 2, C])
        gate = rowb[:, 1, 0:NC * E].rearrange("p (c e) -> p c e", c=NC)
        gate_hi = sb("gate_hi", [P, NC, E], FR)
        gate_lo = sb("gate_lo", [P, NC, E], FR)
        biasb = sb("bias_all", [P, E])
        dec = sb("decay", [P, B, NC])
        wcol = sb("w_col", [P, NC])
        ucol = sb("u_col", [P, NC])
        tf = sb("tf", [P, B])
        tfd = sb("tf_decay", [P, B])
        tfi = sb("tf_scale", [P, B])
        ident = sb("ident", [P, P])
        lower = sb("before", [P, P], F16)
        ones = sb("ones", [P, P], F16)
        iota = sb("iota", [P, E])
        tid = sb("token_id", [P, B * NI])
        blk = sb("blk_mask", [P, EL])
        msk = hr[:, 0:P].rearrange("p (e m) -> p e m", e=EL)
        low8 = sb("low_mask", [P, NS, 8])
        low = sb("low_sum", [P, 8])
        sel = sb("sel", [P, EL, NS], F16)
        slot = sb("dummy_row", [P, NS])
        ex = sb("r_exp", [P, NI, E])
        sc = sb("r_score", [P, NI, E])
        scb = sb("r_biased", [P, NI, E])
        pmx = sb("r_pair_max", [P, NI * G, 2])
        pmn = sb("r_pair_min", [P, NI * G, 2])
        gs = sb("r_group", [P, NI * G])
        g1 = sb("r_group1", [P, NI * G])
        g2 = sb("r_group2", [P, NI * G])
        top = sb("r_top", [P, NI, 8])
        tix = sb("r_top_index", [P, NI, 8], U32)
        geq = sb("r_group_eq", [P, NI, TKG, G])
        eeq = sb("r_expert_eq", [P, NI, K, E], F16)
        mcnt = sb("r_mask_count", [P, E])
        gmask = sb("r_group_mask", [P, NI, G])
        tix16 = sb("r_top_index16", [P, NI, K], F16)
        expert16 = sb("expert_number16", [P, E], F16)
        mask16 = sb("r_mask16", [P, NI, E], F16)
        msum = sb("r_mask_sum", [P, 2, E], F16)
        wsel = sb("r_weight", [P, NI, E])
        wsum = sb("r_weight_sum", [P, NI])
        pint = sb("r_slot", [P, NI, E], I32)
        pa = scb[:, :, :].bitcast(I32)
        pbt = sc[:, :, :].bitcast(I32)
        pa16 = sb("r_slot_a16", [P, NI, E], F16)
        pb16 = sb("r_slot_b16", [P, NI, E], F16)
        oa = sb("onehot_a", [P, NI, NG, SA * EL], F16)
        ob = sb("onehot_b", [P, NI, NG, SB * EL], F16)
        iota16 = sb("iota16", [P, SA, EL], F16)
        tval = db[:, 0:NS * E]
        tgat = sb("t_gather", [P, NS * E], I32)
        tscat = sb("t_scatter", [P, NS * E], I32)
        tzero = db[:, NS * E:2 * NS * E]
        blkbig = nb.rearrange("p (g b e) -> p g b e", g=NG, e=EL)
        dblk = db[:, 2 * NS * E:2 * NS * E + NG * SB].rearrange("p (g b) -> p g b", g=NG)
        lsel = oa[:, 0, :, :].rearrange("p g (a b) -> p g a b", a=8)
        gi = sb("gather_index", [P, 2, NS], I32)
        si = sb("scatter_index", [P, 2, NS], I32)
        wx = sb("slot_weight", [P, RAW, NS])

        bank = [ctx.enter_context(nc.psum_tensor(f"bank{n}", [P, T], FP)) for n in range(8)]
        acc, ring, misc, idxb = bank[0:4], bank[4:6], bank[6], bank[7]
        ybank, tbank = bank[0:2], bank[6:8]

        s_gate, s_gparts, s_cond, s_cst = sem("s_gate"), sem("s_gate_parts"), sem("s_cond"), sem("s_constants")
        s_wdec, s_ubon = sem("s_w_col"), sem("s_u_col")
        s_k = [sem("s_k0"), sem("s_k1")]
        s_r = [sem("s_r0"), sem("s_r1"), sem("s_r2")]
        s_stage = [sem(f"s_stage{n}") for n in range(4)]
        s_swh, s_swl_pool, s_swl_dve = sem("s_shared_hi"), sem("s_shared_lo_by_pool"), sem("s_shared_lo_by_dve")
        s_vec = sem("s_vector_chain")
        s_dexp, s_tfe, s_act = sem("s_decay_exp"), sem("s_tf_exp"), sem("s_scalar_chain")
        s_neg, s_dec = sem("s_tf_neg"), sem("s_decay")
        s_clamp, s_ek, s_eu, s_er = sem("s_clamped"), sem("s_ek"), sem("s_eu"), sem("s_er")
        s_ekv, s_du, s_dv = sem("s_ekv"), sem("s_du"), sem("s_dv")
        s_den, s_rcp = sem("s_den"), sem("s_reciprocal")
        s_flat, s_fhi, s_flo = sem("s_flat"), sem("s_flat_hi"), sem("s_flat_lo")
        s_full, s_free = sem("s_ring_full"), sem("s_ring_free")
        s_rowd = [sem("s_row_stored0"), sem("s_row_stored1")]
        s_lg, s_lgx, s_lgt = sem("s_logits"), sem("s_logits_exp"), sem("s_logits_turned")
        s_mask, s_w, s_wst = sem("s_mask"), sem("s_weights"), sem("s_weights_stored")
        s_pos, s_pint, s_oh, s_ob, s_obt, s_idx = sem("s_pos"), sem("s_pos_read"), sem("s_onehot"), sem("s_onehot_b"), sem("s_onehot_b_numbered"), sem("s_idx")
        s_lsel, s_sel, s_tab = sem("s_lsel"), sem("s_sel"), sem("s_table")
        s_early, s_earlyf = sem("s_early_blocks"), sem("s_early_blocks_copied")
        s_sq, s_hh, s_hl, s_dn = sem("s_square"), sem("s_h_hi"), sem("s_h_lo"), sem("s_down")
        s_acc, s_accf = sem("s_acc"), sem("s_acc_copied")
        s_xr = [sem(f"s_xrow{n}") for n in range(NI)]
        s_out = [sem(f"s_out{n}") for n in range(NI)]
        s_num, s_numdv, s_own = sem("s_num"), sem("s_num_plus_dv"), sem("s_num_times_y")
        s_zero, s_zst = sem("s_zero"), sem("s_zero_stored")
        s_raw = [sem(f"s_raw{n}") for n in range(RAW)]
        s_xg = [sem(f"s_gathered{n}") for n in range(RAW)]
        s_uph, s_upl, s_dnh, s_dnl = sem("s_up_hi"), sem("s_up_lo"), sem("s_down_hi"), sem("s_down_lo")
        s_tr, s_thi, s_tlo, s_wx = sem("s_transposed"), sem("s_xt_hi"), sem("s_xt_lo"), sem("s_slot_weight")
        s_esq, s_ehh, s_ehl = sem("s_e_square"), sem("s_e_hi"), sem("s_e_lo")
        s_yd, s_y = sem("s_y_done"), sem("s_y_scaled")
        s_sc = [sem("s_scattered0"), sem("s_scattered1")]
        s_ix = sem("s_index_copied")
        s_go = sem("s_indirect_may_go")

        NT = B * NC
        EARLY = len(acc)
        NCH = 8
        PER = RAW
        SPLIT_AT = {0: (0, 1), 1: (2,), 2: (3,), 3: (4,), 4: (5,), 5: (6,), 6: (7,)}
        DVE_CHUNKS = (1, 3, 5, 7)
        LOAD_AT = {1: (4, 5), 4: (6,), 5: (7,)}
        SCALE_AT = (0, 1)
        POSTS = {s: ((0, 1), (2, 3), (4, 5), (6, 7)) for s in range(2, B + 1)}
        POSTS[1] = ((0, 1, 2), (3, 4, 5), (6, 7), ())

        def uses(b):
            return (NI + NJ) * b - (EARLY if b > 0 else 0)

        def row_use(b, i):
            return uses(b) + i + (2 if b == 0 else 0)

        def block_use(b, j):
            if b == 0:
                return j - EARLY if j < EARLY + 2 else j
            return uses(b) + NI + j

        def early(j):
            place_ = (oa, ob)[j // 2][:, :, :, :].rearrange("p i g k -> p (i g k)").bitcast(FP)
            return place_[:, (j % 2) * T:(j % 2 + 1) * T]

        def pool_scales(n):
            return n // NC >= 1 and n % NC in SCALE_AT

        def wait(eng, s, v):
            if not isinstance(v, int) or v > 0:
                eng.wait_ge(s, v)

        def chunk(parts_, q):
            up, dn = parts_
            return up[:, q, :] if q < NC else dn[:, 2 * (q - NC):2 * (q - NC) + 2, :].rearrange("p j c -> p (j c)")

        def wait_low(eng, q):
            if q in DVE_CHUNKS:
                eng.wait_ge(s_swl_dve, DVE_CHUNKS.index(q) + 1)
            else:
                eng.wait_ge(s_swl_pool, q + 1 - sum(x < q for x in DVE_CHUNKS))

        def staging(q):
            place_ = fT[:, 1, :, :] if q in (2, 3) else yb
            return place_[:, 2 * (q % 2):2 * (q % 2) + 2, :].rearrange("p a c -> p (a c)")

        def turns(eng, step):
            for e in range(-1, PER):
                step(e, e // PER, e % PER)
            with eng.Fori(1, E // PER - 1) as i:
                for u in range(PER):
                    step(i * PER + u, i, u)
            for e in range(E - PER, E + 1):
                step(e, e // PER, e % PER)

        def has(e, d):
            return not isinstance(e, int) or 0 <= e + d < E

        block = ctx.enter_context(nc.Block())

        @block.sync
        def _(sp):
            def load_tile(n):
                b, c = divmod(n, NC)
                if n >= 2:
                    sp.wait_ge(s_dv, n - 1)
                sp.dma_start(kt[n % 2], kT[c * P:(c + 1) * P, b, :]).then_inc(s_k[n % 2], 16)
                if n >= 3:
                    sp.wait_ge(s_flat, n - 2)
                sp.dma_start(er[n % 3], xT[c * P:(c + 1) * P, b, :]).then_inc(s_r[n % 3], 16)

            def load_stage(q):
                if q >= 4:
                    wait_low(sp, q - 4 if q < 6 else q - 2)
                src = supT[:, q, :] if q < NC else sdownT[:, 2 * (q - NC):2 * (q - NC) + 2, :].rearrange("p j c -> p (j c)")
                sp.dma_start(staging(q), src).then_inc(s_stage[q % 4], 16)

            def rows_of_x(b):
                for i in range(NI):
                    if b == 0:
                        wait_low(sp, NCH - 1)
                    else:
                        sp.wait_ge(s_out[i], 16 * b)
                    sp.dma_start(yb[:, i, :], xrow[b * T + i * P:b * T + (i + 1) * P, :]).then_inc(s_xr[i], 16)

            def results_of(b):
                for i in range(NI):
                    sp.wait_ge(s_accf, NI * b + i + 1)
                    sp.dma_start(out[b * T + i * P:b * T + (i + 1) * P, :], yb[:, i, :]).then_inc(s_out[i], 16)

            sp.dma_start(rowb[:, 0, :], cond.rearrange("b t -> (b t)").partition_broadcast(P)).then_inc(s_cond, 16)
            sp.dma_start(kt[0], kT[0:P, 0, :]).then_inc(s_k[0], 16)
            sp.dma_start(wcol[:, :], wdec).then_inc(s_wdec, 16)
            sp.dma_start(ucol[:, :], ubon).then_inc(s_ubon, 16)
            sp.dma_start(er[0], xT[0:P, 0, :]).then_inc(s_r[0], 16)
            load_tile(1)
            for q in range(4):
                load_stage(q)
            for s in range(B + 1):
                for c in range(NC):
                    n = NC * s + c + 2
                    if n < NT:
                        load_tile(n)
                    if s >= 2 and c == 1:
                        results_of(s - 2)
                    for q in LOAD_AT.get(n - 2, ()):
                        load_stage(q)
                if s == 0:
                    sp.wait_ge(s_zero, 1)
                    sp.dma_start(out[NTOK:NTOK + CAP, :].rearrange("(h p) c -> p h c", h=NS),
                                 hq[:, :, :]).then_inc(s_zst, 16)
                if s >= 1:
                    rows_of_x(s - 1)
                    if s == B:
                        results_of(s - 1)
                if s == B - 1:
                    sp.wait_ge(s_flat, NT)
                    for x in (0, 1):
                        sp.wait_ge(s_rowd[x], 16 * NI * B // 2)
                    for e in range(RAW):
                        sp.dma_start(raw[:, e, 0:UPW], upT[e]).then_inc(s_raw[e], 16)
                        sp.dma_start(raw[:, e, UPW:UPW + DNW], downT[e]).then_inc(s_raw[e], 16)

            with sp.Fori(1, E // RAW) as i:
                for u in range(RAW):
                    sp.wait_ge(s_upl, i * RAW + (u - RAW + 1))
                    sp.dma_start(raw[:, u, 0:UPW], upT[bass.ds(i * RAW + u, 1)].rearrange("o p n -> (o p) n")).then_inc(s_raw[u], 16)
                    sp.wait_ge(s_dnl, i * RAW + (u - RAW + 1))
                    sp.dma_start(raw[:, u, UPW:UPW + DNW], downT[bass.ds(i * RAW + u, 1)].rearrange("o p n -> (o p) n")).then_inc(s_raw[u], 16)

        @block.tensor
        def _(pe):
            def three(dst, lhs, rhs, first, last):
                pe.matmul(dst, lhs[0], rhs[0], start=first, stop=False)
                pe.matmul(dst, lhs[0], rhs[1], start=False, stop=False)
                return pe.matmul(dst, lhs[1], rhs[0], start=False, stop=last)

            def turn_tile(b, i):
                m = row_use(b, i)
                wait(pe, s_free, m - 1)
                for c in range(NC):
                    ins = pe.transpose(ring[m % 2][:, c * P:(c + 1) * P], fT[:, b % 2, c, i * P:(i + 1) * P], ident[:, :])
                ins.then_inc(s_full, 1)

            def first_batch():
                for c in range(NC):
                    flat = [x[0][:, c, :] for x in (flat_hi, flat_lo)]
                    if c == 0:
                        pe.wait_ge(s_gparts, 1)
                    pe.wait_ge(s_flo, c + 1)
                    ins = three(misc[0:E, :], [gate_hi[:, c, :], gate_lo[:, c, :]], flat, c == 0, c == NC - 1)
                    if c == NC - 1:
                        ins.then_inc(s_lg, 1)
                    wait_low(pe, c)
                    for j in range(EARLY):
                        ins = three(acc[j][:, :], [w[:, c, j * P:(j + 1) * P] for w in sup], flat, c == 0, c == NC - 1)
                        if c == NC - 1:
                            ins.then_inc(s_early, 1)

            def turn_rows(b):
                pe.wait_ge(s_flat, NC * (b + 1))
                for i in (0, 1):
                    turn_tile(b, i)
                pe.wait_ge(s_flo, NC * (b + 1))
                pe.wait_ge(s_pint, b)
                for c in range(NC):
                    ins = three(misc[0:E, :], [gate_hi[:, c, :], gate_lo[:, c, :]],
                                [x[b % 2][:, c, :] for x in (flat_hi, flat_lo)], c == 0, c == NC - 1)
                ins.then_inc(s_lg, 1)
                for i in (2, 3):
                    turn_tile(b, i)

            def turn_logits(b):
                pe.wait_ge(s_lgx, b + 1)
                for i in range(NI):
                    ins = pe.transpose(misc[:, i * E:(i + 1) * E], rowb[0:E, 0, i * P:(i + 1) * P], ident[0:E, 0:E])
                ins.then_inc(s_lgt, 1)

            def up(b, j):
                m = block_use(b, j)
                wait(pe, s_free, m - 1)
                for c in range(NC):
                    ins = three(ring[m % 2][:, :], [w[:, c, j * P:(j + 1) * P] for w in sup],
                                [flat_hi[b % 2][:, c, :], flat_lo[b % 2][:, c, :]], c == 0, c == NC - 1)
                ins.then_inc(s_full, 1)

            def down(b, j):
                J = NJ * b + j
                pe.wait_ge(s_hl, J + 1)
                if b == 0 and j % 2 == 0:
                    wait_low(pe, NC + j // 2)
                for i in range(NI):
                    if j == 0 and b == 0:
                        pe.wait_ge(s_earlyf, EARLY)
                    elif j == 0:
                        pe.wait_ge(s_accf, NI * (b - 1) + i + 1)
                    ins = three(acc[i][:, :], [h[:, J % 3, i * P:(i + 1) * P] for h in (hh, hl)],
                                [w[:, j, :] for w in sdn], j == 0, j == NJ - 1)
                    if j == NJ - 1:
                        ins.then_inc(s_acc, 1)
                if j < NJ - 1:
                    ins.then_inc(s_dn, 1)

            def positions(b):
                pe.wait_ge(s_mask, b + 1)
                for i in range(NI):
                    dst = misc[:, P + i * E:P + (i + 1) * E]
                    pe.matmul(dst, lower[:, :], mask16[:, i, :], start=True, stop=False)
                    for before in range(i):
                        pe.matmul(dst, ones[:, :], mask16[:, before, :], start=False, stop=False)
                    ins = pe.matmul(dst, ones[:, :], msum[:, b % 2, :], start=False, stop=True)
                ins.then_inc(s_pos, 1)

            def places(b):
                pe.wait_ge(s_oh, b + 1)
                if b < B - 2:
                    pe.wait_ge(s_obt, b + 1)
                for i in range(NI):
                    for g in range(NG):
                        first, last = b == 0 and i == 0 and g == 0, b == B - 1 and i == NI - 1
                        ins = pe.matmul(idxb[:, g * P:(g + 1) * P],
                                        oa[:, i, g, :], ob[:, i, g, :],
                                        start=first, stop=last and g == NG - 1, skip_group_check=True)
                ins.then_inc(s_idx, 1)

            def table():
                pe.wait_ge(s_lsel, 1)
                for g in range(NG):
                    ins = pe.matmul(misc[:, 2 * P + g * 2 * EL:2 * P + (g + 1) * 2 * EL],
                                    lsel[:, g, :, :].rearrange("p a b -> p (a b)"), sel[:, :, :].rearrange("p e h -> p (e h)"), start=True, stop=True)
                ins.then_inc(s_sel, 1)

            def turn_expert(e, i, u):
                pe.wait_ge(s_xg[u], (i + 1) * 32)
                if isinstance(e, int) and e == 0:
                    pe.wait_ge(s_tab, 1)
                for n in range(2):
                    wait(pe, s_thi, 2 * (e - 1) + n + 1)
                    wait(pe, s_tlo, 2 * (e - 1) + n + 1)
                    for c in (2 * n, 2 * n + 1):
                        for h in range(NS):
                            o = (c % 2) * CAP + h * P
                            ins = pe.transpose(tbank[n][:, o:o + P], xe[:, u, h, c * P:(c + 1) * P], ident[:, :])
                    ins.then_inc(s_tr, 1)

            def expert_weights(u, dn):
                if dn:
                    return [parts[u % 2][:, x, UPW:UPW + DNW].rearrange("p (h c) -> p h c", h=NH) for x in (0, 1)]
                return [parts[u % 2][:, x, 0:UPW].rearrange("p (c h) -> p c h", c=NC) for x in (0, 1)]

            def expert_up(e, u):
                pe.wait_ge(s_tlo, 2 * e + 2)
                pe.wait_ge(s_upl, e + 1)
                pe.wait_ge(s_free, uses(B) + e - 1)
                w = expert_weights(u, False)
                for hb in range(NH):
                    for c in range(NC):
                        ins = three(ring[u % 2][:, hb * CAP:(hb + 1) * CAP], [x[:, c, hb * P:(hb + 1) * P] for x in w],
                                    [x[:, c, :] for x in xt[u % 2]], c == 0, c == NC - 1)
                ins.then_inc(s_full, 1)

            def expert_down(e, u):
                pe.wait_ge(s_ehl, e + 1)
                pe.wait_ge(s_dnl, e + 1)
                w = expert_weights(u, True)
                for h in range(NS):
                    if isinstance(e, int) and e == 0:
                        pe.wait_ge(s_accf, NI * B)
                    wait(pe, s_y, 2 * (e - 1) + h + 1)
                    for hb in range(NH):
                        ins = three(ybank[h][:, :], [x[:, u % 2, hb * CAP + h * P:hb * CAP + (h + 1) * P] for x in (hh, hl)],
                                    [x[:, hb, :] for x in w], hb == 0, hb == NH - 1)
                    ins.then_inc(s_yd, 1)

            for b in range(B):
                ahead = 2 + (EARLY if b == 0 else 0)
                if b == 0:
                    first_batch()
                else:
                    turn_rows(b)
                up(b, ahead - 2)
                up(b, ahead - 1)
                if b == 0:
                    pe.wait_ge(s_cst, 1)
                turn_logits(b)
                for j in range(NJ):
                    if b == 0 and j in (EARLY, EARLY + 1):
                        turn_tile(0, 2 * (j - EARLY))
                        turn_tile(0, 2 * (j - EARLY) + 1)
                    if b > 0 and j + 2 < NJ:
                        up(b, j + 2)
                    if b == 0 and j == EARLY + 1:
                        up(b, NJ - 2)
                        up(b, NJ - 1)
                    down(b, j)
                    if b >= 1 and j == (2 if b < B - 1 else 0):
                        places(b - 1)
                    if b < B - 1 and j == 5:
                        positions(b)
                    if b == B - 1:
                        if j == 1:
                            positions(b)
                        if j == 2:
                            places(b)
                        if j == 3:
                            table()
                        if j == NJ - 2:
                            turn_expert(0, 0, 0)

            def step(e, i, u):
                if has(e, 1) and not (isinstance(e, int) and e < 0):
                    turn_expert(e + 1, i + (u + 1) // PER, (u + 1) % PER)
                if has(e, 0):
                    expert_up(e, u)
                if has(e, -1):
                    expert_down(e - 1, (u - 1) % PER)

            turns(pe, step)

        @block.scalar
        def _(act):
            chain = [0]

            def link(ins):
                chain[0] += 1
                ins.then_inc(s_act, 1)
                return chain[0]

            act.preload_act_table_set("natural_log_exp_and_others")
            act.dma_start(gate, gateT).then_inc(s_gate, 16)
            act.dma_start(biasb[:, :], bias.partition_broadcast(P)).then_inc(s_gate, 16)
            act.wait_ge(s_wdec, 16)
            act.wait_ge(s_act, link(act.activation(wcol[:, :], wcol[:, :], ACT.Exp)))
            act.activation(wcol[:, :], wcol[:, :], ACT.Exp, scale=-1.0).then_inc(s_dexp, 1)
            act.wait_ge(s_neg, 1)
            act.activation(tf[:, :], tf[:, :], ACT.Exp).then_inc(s_tfe, 1)

            def exps(n):
                act.wait_ge(s_clamp, 2 * n + 1)
                act.activation(ek[n % 2], ek[n % 2], ACT.Exp).then_inc(s_ek, 1)
                act.wait_ge(s_clamp, 2 * n + 2)
                act.activation(eu[n % 2], eu[n % 2], ACT.Exp).then_inc(s_eu, 1)
                act.wait_ge(s_r[n % 3], 16 * (n // 3 + 1))
                act.wait_ge(s_act, link(act.activation(er[n % 3], er[n % 3], ACT.Exp, scale=-1.0)))
                if n == 0:
                    act.wait_ge(s_dec, 1)
                b = n // NC
                act.activation(er[n % 3], er[n % 3], ACT.Identity, bias=tfi[:, b:b + 1], scale=tfi[:, b:b + 1]).then_inc(s_er, 1)

            def reciprocal(n):
                act.wait_ge(s_den, n + 1)
                act.wait_ge(s_act, link(act.activation(er[n % 3], den[n % 2], ACT.Ln)))
                act.activation(er[n % 3], er[n % 3], ACT.Exp, scale=-1.0).then_inc(s_rcp, 1)

            def flat_high(n):
                b, c = divmod(n, NC)
                act.wait_ge(s_flat, n + 1)
                if b >= 2:
                    act.wait_ge(s_full, uses(b - 1))
                act.activation(flat_hi[b % 2][:, c, :], fT[:, b % 2, c, :], ACT.Copy).then_inc(s_fhi, 1)

            def shared_weights_high(q):
                act.wait_ge(s_stage[q % 4], 16 * (q // 4 + 1))
                act.activation(chunk((sup[0], sdn[0]), q), staging(q), ACT.Copy).then_inc(s_swh, 1)

            def post(J):
                b, j = divmod(J, NJ)
                relu = hr[:, :]
                if J < EARLY:
                    relu = early(J)
                    act.wait_ge(s_earlyf, J + 1)
                else:
                    m = block_use(b, j)
                    act.wait_ge(s_full, m + 1)
                    act.wait_ge(s_sq, J)
                    act.activation(relu, ring[j % 2][:, :], ACT.Relu).then_inc(s_free, 1)
                    act.wait_ge(s_free, m + 1)
                wait(act, s_hl, J - 1)
                if J == 0:
                    act.wait_ge(s_zst, 16)
                act.activation(hq[:, J % 2, :], relu, ACT.Square).then_inc(s_sq, 1)
                act.wait_ge(s_sq, J + 1)
                if J >= 3:
                    last = J - 3
                    if last % NJ == NJ - 1:
                        act.wait_ge(s_acc, NI * (last // NJ + 1))
                    else:
                        act.wait_ge(s_dn, last - last // NJ + 1)
                act.activation(hh[:, J % 3, :], hq[:, J % 2, :], ACT.Copy).then_inc(s_hh, 1)

            def number_onehots(b):
                act.wait_ge(s_ob, b + 1)
                for i in range(NI):
                    ins = act.activation(ob[:, i, :, :].rearrange("p g k -> p (g k)"), ob[:, i, :, :].rearrange("p g k -> p (g k)"),
                                         ACT.Copy, scale=tid[:, b * NI + i:b * NI + i + 1])
                ins.then_inc(s_obt, 1)

            def early_blocks():
                for j in range(EARLY):
                    act.wait_ge(s_early, j + 1)
                    act.activation(early(j), acc[j][:, :], ACT.Relu).then_inc(s_earlyf, 1)

            def rows_out(b, tiles=range(NI)):
                for i in tiles:
                    t = NI * b + i
                    act.wait_ge(s_full, row_use(b, i) + 1)
                    if t >= 2:
                        act.wait_ge(s_rowd[t % 2], 16 * (t // 2))
                        if i == 0:
                            act.wait_ge(s_lgt, b)
                    elif t == 0:
                        act.wait_ge(s_lgt, 1)
                    else:
                        act.wait_ge(s_gparts, 1)
                    act.activation(rowb[:, t % 2, :], ring[i % 2][:, :], ACT.Copy).then_inc(s_free, 1)
                    act.wait_ge(s_free, row_use(b, i) + 1)
                    act.dma_start(rows[t * P:(t + 1) * P, 0:C], rowb[:, t % 2, :]).then_inc(s_rowd[t % 2], 16)

            def logits_out(b):
                act.wait_ge(s_lg, b + 1)
                if b == 0:
                    act.wait_ge(s_neg, 1)
                else:
                    act.wait_ge(s_rowd[0], 16 * (NI * (b + 1) // 2))
                act.activation(rowb[0:E, 0, :], misc[0:E, :], ACT.Exp, scale=-1.0).then_inc(s_lgx, 1)

            def up_high(e, i, u):
                act.wait_ge(s_raw[u], (i + 1) * 32)
                if isinstance(e, int) and e < 2:
                    act.wait_ge(s_full, uses(B - 1 + e))
                else:
                    act.wait_ge(s_full, uses(B) + e - 1)
                act.activation(parts[u % 2][:, 0, 0:UPW], raw[:, u, 0:UPW], ACT.Copy).then_inc(s_uph, 1)

            def down_high(e, u):
                if not (isinstance(e, int) and e < 2):
                    act.wait_ge(s_yd, 2 * e - 2)
                act.activation(parts[u % 2][:, 0, UPW:UPW + DNW], raw[:, u, UPW:UPW + DNW], ACT.Copy).then_inc(s_dnh, 1)

            def xt_high(e, u):
                for n in range(2):
                    act.wait_ge(s_tr, 2 * e + n + 1)
                    if not (isinstance(e, int) and e == 0):
                        act.wait_ge(s_full, uses(B) + e - 1)
                    act.activation(xt[u % 2][0][:, 2 * n:2 * n + 2, :].rearrange("p c s -> p (c s)"), tbank[n][:, :],
                                   ACT.Copy).then_inc(s_thi, 1)

            def expert_square(e, u):
                act.wait_ge(s_full, uses(B) + e + 1)
                if isinstance(e, int) and e == 0:
                    act.wait_ge(s_sq, NJ * B)
                else:
                    act.wait_ge(s_esq, e)
                act.activation(hr[:, :], ring[u % 2][:, :], ACT.Relu).then_inc(s_free, 1)
                act.wait_ge(s_free, uses(B) + e + 1)
                if isinstance(e, int) and e < 2:
                    act.wait_ge(s_hl, NJ * B)
                else:
                    act.wait_ge(s_ehl, e - 1)
                act.activation(hq[:, u % 2, :], hr[:, :], ACT.Square).then_inc(s_esq, 1)

            def results(e, i, u):
                act.wait_ge(s_wx, e + 1)
                if isinstance(e, int) and e < 2:
                    for x in range(NI):
                        act.wait_ge(s_out[x], 16 * B)
                else:
                    act.wait_ge(s_sc[u % 2], (2 * i + u // 2) * 32)
                for h in range(NS):
                    act.wait_ge(s_yd, 2 * e + h + 1)
                    act.activation(yb[:, 2 * (u % 2) + h, :], ybank[h][:, :], ACT.Copy,
                                   scale=wx[:, u, h:h + 1]).then_inc(s_y, 1)

            exps(0)
            for s in range(B + 1):
                for c in range(NC):
                    n = NC * s + c
                    if n == 2 * NC - 1:
                        reciprocal(n)
                    if n + 1 < NT:
                        exps(n + 1)
                    for q in SPLIT_AT.get(n, ()):
                        shared_weights_high(q)
                    if s >= 1 and c == 0:
                        if s > 1:
                            flat_high(n - 1)
                        if n < NT:
                            reciprocal(n)
                        if s == 1:
                            early_blocks()
                        else:
                            rows_out(s - 1)
                        logits_out(s - 1)
                    if 2 <= s < B and c == 1:
                        number_onehots(s - 2)
                    if s == 1 and c == 2:
                        reciprocal(n)
                        rows_out(0, (2, 3))
                    if s >= 1:
                        for j in POSTS[s][c][:1]:
                            post(NJ * (s - 1) + j)
                    if (c >= 1 or s == 0) and not (s == 1 and c >= 2):
                        if n < NT:
                            reciprocal(n)
                    if s >= 1:
                        for j in POSTS[s][c][1:]:
                            post(NJ * (s - 1) + j)
                    if s == 1 and c == 1:
                        rows_out(0, (0, 1))
                    if s == B and c == 2:
                        up_high(0, 0, 0)
                    if c >= 1 and n < NT:
                        flat_high(n - 1)
                    if n == NC - 1:
                        flat_high(n)

            def step(e, i, u):
                if has(e, 1) and not (isinstance(e, int) and e < 0):
                    up_high(e + 1, i + (u + 1) // PER, (u + 1) % PER)
                if has(e, 0):
                    down_high(e, u)
                if has(e, 1):
                    xt_high(e + 1, (u + 1) % PER)
                if has(e, 0):
                    expert_square(e, u)
                if has(e, -1):
                    results(e - 1, i + (u - 1) // PER, (u - 1) % PER)

            turns(act, step)

        @block.vector
        def _(dve):
            chain = [0]

            def link(ins):
                chain[0] += 1
                ins.then_inc(s_vec, 1)
                return chain[0]

            def tt(o, a, b_, op):
                return link(dve.tensor_tensor(o, a, b_, op))

            def after(n):
                dve.wait_ge(s_vec, n)

            dve.wait_ge(s_cond, 16)
            after(link(dve.tensor_reduce(tf[:, :], rowb[:, 0, :].rearrange("p (b t) -> p b t", b=B), AX.X, ALU.add)))
            dve.tensor_scalar(tf[:, :], tf[:, :], -1.0, 80.0, ALU.mult, ALU.min).then_inc(s_neg, 1)

            def clamp(n):
                dve.wait_ge(s_k[n % 2], 16 * (n // 2 + 1))
                if n >= 2:
                    dve.wait_ge(s_dv, n - 1)
                dve.tensor_scalar(ek[n % 2], kt[n % 2], KLIM, None, ALU.min).then_inc(s_clamp, 1)
                if n == 0:
                    dve.wait_ge(s_ubon, 16)
                dve.tensor_scalar(eu[n % 2], kt[n % 2], ucol[:, n % NC:n % NC + 1], KLIM, ALU.add,
                                  ALU.min).then_inc(s_clamp, 1)

            clamp(0)
            dve.wait_ge(s_tfe, 1)
            after(link(dve.tensor_scalar(tf[:, :], tf[:, :], 1.0, None, ALU.add)))
            after(link(dve.reciprocal(tf[:, :], tf[:, :])))
            n0 = link(dve.tensor_scalar(tfi[:, :], tf[:, :], 0.2, 0.8, ALU.mult, ALU.add))
            n1 = link(dve.tensor_scalar(tfd[:, :], tf[:, :], 0.5, 0.5, ALU.mult, ALU.add))
            after(n0)
            dve.reciprocal(tfi[:, :], tfi[:, :]).then_inc(s_dec, 1)
            dve.wait_ge(s_dexp, 1)
            after(n1)
            for b in range(B):
                n0 = link(dve.tensor_scalar(dec[:, b, :], wcol[:, :], tfd[:, b:b + 1], None, ALU.mult))
            link(dve.memset(msum[:, 0, :], 0.0))
            after(n0)

            def gate_parts():
                dve.wait_ge(s_gate, 32)
                after(link(dve.tensor_copy(gate_hi[:, :, :], gate)))
                dve.tensor_tensor(gate_lo[:, :, :], gate, gate_hi[:, :, :].bitcast(FP), ALU.subtract).then_inc(s_gparts, 1)

            def wkv(n):
                b, c = divmod(n, NC)
                d = dec[:, b, c:c + 1].to_broadcast([P, T])
                e_, v_, nf, df = ek[n % 2], ekv[n % 2], num[n % 2], den[n % 2]
                if n + 1 < NT:
                    clamp(n + 1)
                if n == NC:
                    dve.wait_ge(s_fhi, NC)
                    dve.wait_ge(s_flo, NC - 1)
                    dve.tensor_tensor(flat_lo[0][:, NC - 1, :], fT[:, 0, NC - 1, :], flat_hi[0][:, NC - 1, :].bitcast(FP),
                                      ALU.subtract).then_inc(s_flo, 1)
                if n >= 2:
                    dve.wait_ge(s_flat, n - 1)
                old = n - 1 if n >= 1 and n != NC else None
                dve.wait_ge(s_ek, n + 1)
                link(dve.tensor_tensor_scan(df, d, e_, 0.0, ALU.mult, ALU.add))
                a2 = link(dve.tensor_tensor_scan(db[:, ::-1], d, e_[:, ::-1], 0.0, ALU.mult, ALU.add))
                if old is not None:
                    o1 = den_times_y(old)
                    if c == 0:
                        num_times_y(old)
                after(a2)
                a3 = tt(df, df, db, ALU.add)
                if old is not None and c == 0:
                    newton(old, o1)
                elif old is not None:
                    num_times_y(old)
                dve.wait_ge(s_du, n + 1)
                after(a3)
                a4 = tt(df, df, eu[n % 2], ALU.add)
                if old is not None and c > 0:
                    newton(old, o1)
                dve.wait_ge(s_er, n + 1)
                after(a4)
                dve.scalar_tensor_tensor(out=df, in0=df, scalar=1e-8, in1=er[n % 3], op0=ALU.max, op1=ALU.mult).then_inc(s_den, 1)
                dve.wait_ge(s_ekv, n + 1)
                link(dve.tensor_tensor_scan(nf, d, v_, 0.0, ALU.mult, ALU.add))
                a5 = link(dve.tensor_tensor_scan(nb[:, ::-1], d, v_[:, ::-1], 0.0, ALU.mult, ALU.add))
                after(a5)
                dve.tensor_tensor(nf, nf, nb, ALU.add).then_inc(s_num, 1)
                if n == NC - 1:
                    divide(n)

            def shared_weights_low(q):
                dve.wait_ge(s_swh, q + 1)
                dve.tensor_tensor(chunk((sup[1], sdn[1]), q), staging(q), chunk((sup[0], sdn[0]), q).bitcast(FP),
                                  ALU.subtract).then_inc(s_swl_dve, 1)

            def den_times_y(n):
                dve.wait_ge(s_rcp, n + 1)
                return link(dve.scalar_tensor_tensor(out=den[n % 2], in0=den[n % 2], scalar=3e38, in1=er[n % 3],
                                                     op0=ALU.min, op1=ALU.mult))

            def num_times_y(n):
                if not pool_scales(n):
                    dve.wait_ge(s_numdv, n + 1)
                    dve.tensor_tensor(num[n % 2], num[n % 2], er[n % 3], ALU.mult).then_inc(s_own, 1)

            def newton(n, den_y):
                b, c = divmod(n, NC)
                if b >= 2:
                    dve.wait_ge(s_flo, NC * (b - 1))
                    dve.wait_ge(s_full, uses(b - 1))
                if n in (NC, NC + 2):
                    wait_low(dve, 2 + (n - NC) // 2)
                after(den_y)
                dve.wait_ge(s_own, n + 1)
                dve.scalar_tensor_tensor(out=fT[:, b % 2, c, :], in0=den[n % 2], scalar=2.0, in1=num[n % 2],
                                         op0=ALU.subtract, op1=ALU.mult, reverse0=True).then_inc(s_flat, 1)

            def divide(n):
                den_y = den_times_y(n)
                num_times_y(n)
                newton(n, den_y)

            def sum_out(b, i):
                dve.wait_ge(s_xr[i], 16 * (b + 1))
                dve.wait_ge(s_acc, NI * b + i + 1)
                dve.tensor_tensor(yb[:, i, :], acc[i][:, :], yb[:, i, :], ALU.add).then_inc(s_accf, 1)

            def choose(b):
                dve.wait_ge(s_lgt, b + 1)
                if b == 0:
                    dve.wait_ge(s_gate, 32)
                    dve.wait_ge(s_cst, 1)
                if b >= 1:
                    dve.wait_ge(s_wst, 16 * b)
                    dve.wait_ge(s_pos, b)
                flat = lambda x: x[:, :, :].rearrange("p i e -> p (i e)")
                after(link(dve.tensor_scalar(flat(ex), misc[:, 0:NI * E], 1.0, None, ALU.add)))
                after(link(dve.reciprocal(flat(sc), flat(ex))))
                after(tt(scb[:, :, :], sc[:, :, :], biasb[:, None, :].to_broadcast([P, NI, E]), ALU.add))
                pair = flat(scb).rearrange("p (g q x) -> p g q x", q=2, x=2)
                tt(pmx[:, :, :], pair[:, :, :, 0], pair[:, :, :, 1], ALU.max)
                after(tt(pmn[:, :, :], pair[:, :, :, 0], pair[:, :, :, 1], ALU.min))
                tt(g1[:, :], pmx[:, :, 0], pmx[:, :, 1], ALU.min)
                tt(g2[:, :], pmn[:, :, 0], pmn[:, :, 1], ALU.max)
                after(tt(gs[:, :], pmx[:, :, 0], pmx[:, :, 1], ALU.max))
                after(tt(g1[:, :], g1[:, :], g2[:, :], ALU.max))
                after(tt(gs[:, :], gs[:, :], g1[:, :], ALU.add))
                for i in range(NI):
                    last = link(dve.max(top[:, i, :], gs[:, i * G:(i + 1) * G]))
                after(last)
                for i in range(NI):
                    last = link(dve.max_index(tix[:, i, :], top[:, i, :], gs[:, i * G:(i + 1) * G]))
                after(last)
                after(tt(geq[:, :, :, :], tix[:, :, 0:TKG][:, :, :, None].to_broadcast([P, NI, TKG, G]),
                         iota[:, 0:G][:, None, None, :].to_broadcast([P, NI, TKG, G]), ALU.is_equal))
                after(link(dve.tensor_reduce(gmask[:, :, :], geq[:, :, :, :].rearrange("p i k g -> p i g k"), AX.X, ALU.add)))
                after(tt(ex[:, :, :].rearrange("p i (g x) -> p (i g) x", x=EG), scb[:, :, :].rearrange("p i (g x) -> p (i g) x", x=EG),
                         gmask[:, :, :].rearrange("p i g -> p (i g)")[:, :, None].to_broadcast([P, NI * G, EG]), ALU.mult))
                for i in range(NI):
                    last = link(dve.max(top[:, i, :], ex[:, i, :]))
                after(last)
                for i in range(NI):
                    last = link(dve.max_index(tix[:, i, :], top[:, i, :], ex[:, i, :]))
                after(last)
                after(link(dve.tensor_copy(tix16[:, :, :], tix[:, :, 0:K])))
                after(tt(eeq[:, :, :, :], tix16[:, :, :][:, :, :, None].to_broadcast([P, NI, K, E]),
                         expert16[:, :][:, None, None, :].to_broadcast([P, NI, K, E]), ALU.is_equal))
                after(tt(eeq[:, :, 0:2, :], eeq[:, :, 0:2, :], eeq[:, :, 2:4, :], ALU.add))
                dve.tensor_tensor(mask16[:, :, :], eeq[:, :, 0, :], eeq[:, :, 1, :], ALU.add).then_inc(s_mask, 1)
                dve.wait_ge(s_mask, b + 1)
                after(tt(wsel[:, :, :], sc[:, :, :], mask16[:, :, :], ALU.mult))
                after(link(dve.tensor_reduce(wsum[:, :], wsel[:, :, :], AX.X, ALU.add)))
                if b < B - 1:
                    link(dve.tensor_reduce(mcnt[:, :], mask16[:, :, :].rearrange("p i e -> p e i"), AX.X, ALU.add))
                after(link(dve.tensor_scalar(wsum[:, :], wsum[:, :], 1e-20, None, ALU.add)))
                after(link(dve.reciprocal(wsum[:, :], wsum[:, :])))
                if b < B - 1:
                    tt(msum[:, (b + 1) % 2, :], msum[:, b % 2, :], mcnt[:, :], ALU.add)
                after(tt(wsel[:, :, :], wsel[:, :, :], wsum[:, :, None].to_broadcast([P, NI, E]), ALU.mult))
                dve.tensor_scalar(wsel[:, :, :], wsel[:, :, :], SCALE, None, ALU.mult).then_inc(s_w, 1)

            def place(b):
                def filler(i):
                    if b < B - 1:
                        sum_out(b, i)

                def onehot(o, v, count):
                    return dve.tensor_tensor(
                        o[:, :, :, :].rearrange("p i g (a e) -> p (i g) a e", a=count),
                        v[:, :, :].rearrange("p i (g e) -> p (i g) e", g=NG)[:, :, None, :].to_broadcast([P, NI * NG, count, EL]),
                        iota16[:, None, :, :].to_broadcast([P, NI * NG, count, EL]), ALU.is_equal)

                dve.wait_ge(s_pos, b + 1)
                if b == 0:
                    dve.wait_ge(s_sq, EARLY)
                else:
                    dve.wait_ge(s_idx, b)
                pos = misc[:, P:P + NI * E].rearrange("p (i e) -> p i e", i=NI)
                dve.scalar_tensor_tensor(out=ex[:, :, :], in0=pos, scalar=1.0, in1=mask16[:, :, :],
                                         op0=ALU.add, op1=ALU.mult).then_inc(s_pint, 1)
                filler(0)
                dve.wait_ge(s_pint, b + 1)
                whole = link(dve.tensor_scalar(pint[:, :, :], ex[:, :, :], 1.0, None, ALU.subtract))
                filler(1)
                after(whole)
                link(dve.tensor_scalar(pa, pint[:, :, :], 4, None, ALU.arith_shift_right))
                digits = link(dve.tensor_scalar(pbt, pint[:, :, :], SB - 1, None, ALU.bitwise_and))
                filler(2)
                after(digits)
                link(dve.tensor_copy(pa16[:, :, :], pa))
                digits16 = link(dve.tensor_copy(pb16[:, :, :], pbt))
                filler(3)
                after(digits16)
                onehot(ob, pb16, SB).then_inc(s_ob, 1)
                if b >= B - 2:
                    link(onehot(oa, pa16, SA))
                    dve.wait_ge(s_ob, b + 1)
                    for i in range(NI):
                        last = link(dve.tensor_scalar(ob[:, i, :, :], ob[:, i, :, :], tid[:, b * NI + i:b * NI + i + 1], None, ALU.mult))
                    after(last)
                    dve.sem_inc(s_oh, 1)
                else:
                    onehot(oa, pa16, SA).then_inc(s_oh, 1)

            def make_table():
                dve.wait_ge(s_idx, B)
                after(tt(blkbig, idxb[:, :].rearrange("p (g b e) -> p g b e", g=NG, e=EL),
                         blk[:, None, None, :].to_broadcast([P, NG, SB, EL]), ALU.mult))
                after(link(dve.tensor_reduce(dblk, blkbig, AX.X, ALU.add)))
                dve.tensor_tensor(lsel, dblk[:, :, None, :].to_broadcast([P, NG, 8, SB]),
                                  low[:, None, :, None].to_broadcast([P, NG, 8, SB]), ALU.mult).then_inc(s_lsel, 1)
                dve.wait_ge(s_sel, 1)
                after(link(dve.tensor_copy(tval, misc[:, 2 * P:2 * P + NS * E])))
                after(link(dve.tensor_scalar(tzero, tval, 0.0, None, ALU.is_equal)))
                link(dve.tensor_scalar(tgat[:, :], tval, 1.0, 0.0, ALU.subtract, ALU.max))
                after(tt(tzero.rearrange("p (e h) -> p e h", h=NS), tzero.rearrange("p (e h) -> p e h", h=NS),
                         slot[:, None, :].to_broadcast([P, E, NS]), ALU.mult))
                dve.scalar_tensor_tensor(out=tscat[:, :], in0=tval, scalar=-1.0, in1=tzero,
                                         op0=ALU.add, op1=ALU.add).then_inc(s_tab, 1)

            for s in range(B):
                for c in range(NC):
                    wkv(NC * s + c)
                    if s == 0 and c == 0:
                        gate_parts()
                    for q in SPLIT_AT.get(NC * s + c, ()):
                        if q in DVE_CHUNKS:
                            shared_weights_low(q)
                    if s >= 2 and c == 0:
                        place(s - 2)
                    if s >= 1 and c == 1:
                        choose(s - 1)
            divide(NT - 1)
            place(B - 2)
            choose(B - 1)
            place(B - 1)
            make_table()

            def up_low(e, u):
                dve.wait_ge(s_uph, e + 1)
                dve.tensor_tensor(parts[u % 2][:, 1, 0:UPW], raw[:, u, 0:UPW],
                                  parts[u % 2][:, 0, 0:UPW].bitcast(FP), ALU.subtract).then_inc(s_upl, 1)

            def down_low(e, u):
                dve.wait_ge(s_dnh, e + 1)
                dve.tensor_tensor(parts[u % 2][:, 1, UPW:UPW + DNW], raw[:, u, UPW:UPW + DNW],
                                  parts[u % 2][:, 0, UPW:UPW + DNW].bitcast(FP), ALU.subtract).then_inc(s_dnl, 1)

            def split_h(e, u):
                dve.wait_ge(s_esq, e + 1)
                if not (isinstance(e, int) and e < 2):
                    dve.wait_ge(s_yd, 2 * e - 2)
                dve.tensor_copy(hh[:, u % 2, :], hq[:, u % 2, :]).then_inc(s_ehh, 1)
                dve.wait_ge(s_ehh, e + 1)
                dve.tensor_tensor(hl[:, u % 2, :], hq[:, u % 2, :], hh[:, u % 2, :].bitcast(FP), ALU.subtract).then_inc(s_ehl, 1)

            def xt_low(e, i, u):
                dve.wait_ge(s_xg[u], (i + 1) * 32)
                if not (isinstance(e, int) and e < RAW):
                    dve.wait_ge(s_y, 2 * (e - RAW + 1))
                dve.tensor_copy(wx[:, u, :][:, :, None], xe[:, u, :, bass.ds(e + C, 1)]).then_inc(s_wx, 1)
                for n in range(2):
                    dve.wait_ge(s_thi, 2 * e + n + 1)
                    dve.tensor_tensor(xt[u % 2][1][:, 2 * n:2 * n + 2, :].rearrange("p c s -> p (c s)"), tbank[n][:, :],
                                      xt[u % 2][0][:, 2 * n:2 * n + 2, :].rearrange("p c s -> p (c s)").bitcast(FP),
                                      ALU.subtract).then_inc(s_tlo, 1)

            def step(e, i, u):
                if has(e, 1):
                    up_low(e + 1, (u + 1) % PER)
                if has(e, 0):
                    down_low(e, u)
                if has(e, 1):
                    xt_low(e + 1, i + (u + 1) // PER, (u + 1) % PER)
                if has(e, 0):
                    split_h(e, u)
                if isinstance(e, int) and e == -1:
                    for x in range(NI):
                        sum_out(B - 1, x)

            turns(dve, step)

        @block.gpsimd
        def _(pl):
            def wkv(n):
                if n > NC + 1 and n % NC == 1:
                    flat_low(n - 2)
                pl.wait_ge(s_ek, n + 1)
                pl.tensor_tensor(ekv[n % 2], ek[n % 2], kt[n % 2], ALU.mult).then_inc(s_ekv, 1)
                pl.wait_ge(s_eu, n + 1)
                pl.tensor_tensor(eu[n % 2], eu[n % 2], ek[n % 2], ALU.subtract).then_inc(s_du, 1)
                pl.wait_ge(s_du, n + 1)
                pl.tensor_tensor(dv[n % 2], eu[n % 2], kt[n % 2], ALU.mult).then_inc(s_dv, 1)

            def add_own(n):
                pl.wait_ge(s_num, n + 1)
                pl.tensor_tensor(num[n % 2], num[n % 2], dv[n % 2], ALU.add).then_inc(s_numdv, 1)
                if pool_scales(n):
                    pl.wait_ge(s_rcp, n + 1)
                    pl.wait_ge(s_numdv, n + 1)
                    pl.wait_ge(s_own, n)
                    pl.tensor_tensor(num[n % 2], num[n % 2], er[n % 3], ALU.mult).then_inc(s_own, 1)

            def flat_low(n):
                b, c = divmod(n, NC)
                pl.wait_ge(s_fhi, n + 1)
                if n == NC:
                    pl.wait_ge(s_flo, NC)
                pl.tensor_tensor(flat_lo[b % 2][:, c, :], fT[:, b % 2, c, :], flat_hi[b % 2][:, c, :].bitcast(FP),
                                 ALU.subtract).then_inc(s_flo, 1)

            def h_low(J):
                pl.wait_ge(s_hh, J + 1)
                pl.tensor_tensor(hl[:, J % 3, :], hq[:, J % 2, :], hh[:, J % 3, :].bitcast(FP), ALU.subtract).then_inc(s_hl, 1)

            def shared_weights_low(q):
                pl.wait_ge(s_swh, q + 1)
                pl.tensor_tensor(chunk((sup[1], sdn[1]), q), staging(q), chunk((sup[0], sdn[0]), q).bitcast(FP),
                                 ALU.subtract).then_inc(s_swl_pool, 1)

            def store_weights(b):
                pl.wait_ge(s_w, b + 1)
                pl.dma_start(rows[b * T:(b + 1) * T, C:C + E].rearrange("(i p) e -> p i e", p=P), wsel[:, :, :]).then_inc(s_wst, 16)

            n = [0]

            def seq(ins):
                n[0] += 1
                ins.then_inc(s_ix, 1)
                pl.wait_ge(s_ix, n[0])

            seq(pl.memset(ident[:, :], 0.0))
            seq(pl.affine_select(out=ident[:, :], in_=ident[:, :], compare_op=ALU.not_equal, fill=1.0, base=0,
                                 pattern=[[-1, P]], channel_multiplier=1))
            seq(pl.memset(ones[:, :], 1.0))
            seq(pl.affine_select(out=lower[:, :], in_=ones[:, :], compare_op=ALU.is_gt, fill=0.0, base=0,
                                 pattern=[[1, P]], channel_multiplier=-1))
            seq(pl.iota(iota[:, :], pattern=[[1, E]], base=0, channel_multiplier=0, allow_small_or_imprecise_dtypes=True))
            seq(pl.iota(expert16[:, :], pattern=[[1, E]], base=0, channel_multiplier=0, allow_small_or_imprecise_dtypes=True))
            seq(pl.iota(tid[:, :], pattern=[[P, B * NI]], base=1, channel_multiplier=1, allow_small_or_imprecise_dtypes=True))
            seq(pl.iota(slot[:, :], pattern=[[P, NS]], base=NTOK + 1, channel_multiplier=1, allow_small_or_imprecise_dtypes=True))
            seq(pl.iota(iota16[:, :, :], pattern=[[1, SA], [0, EL]], base=0, channel_multiplier=0, allow_small_or_imprecise_dtypes=True))
            seq(pl.memset(msk[:, :, :], 0.0))
            seq(pl.affine_select(out=msk[:, :, :], in_=msk[:, :, :], compare_op=ALU.not_equal, fill=1.0, base=0,
                                 pattern=[[-1, EL], [-EL, P // EL]], channel_multiplier=1))
            for half in (8, 4, 2):
                seq(pl.tensor_tensor(msk[:, :, 0:half], msk[:, :, 0:half], msk[:, :, half:2 * half], ALU.add))
            seq(pl.tensor_tensor(blk[:, :, None], msk[:, :, 0:1], msk[:, :, 1:2], ALU.add))
            seq(pl.tensor_copy(sel[:, :, :], blk[:, :, None].to_broadcast([P, EL, NS])))
            seq(pl.affine_select(out=sel[:, :, :], in_=sel[:, :, :], compare_op=ALU.is_ge, fill=0.0, base=0,
                                 pattern=[[0, EL], [-P // NS, NS]], channel_multiplier=1))
            seq(pl.affine_select(out=sel[:, :, :], in_=sel[:, :, :], compare_op=ALU.is_gt, fill=0.0, base=P // NS,
                                 pattern=[[0, EL], [P // NS, NS]], channel_multiplier=-1))
            seq(pl.memset(low8[:, :, :], 1.0))
            seq(pl.affine_select(out=low8[:, :, :], in_=low8[:, :, :], compare_op=ALU.is_ge, fill=0.0, base=0,
                                 pattern=[[-P // NS, NS], [-8, 8]], channel_multiplier=1))
            seq(pl.affine_select(out=low8[:, :, :], in_=low8[:, :, :], compare_op=ALU.is_gt, fill=0.0, base=8,
                                 pattern=[[P // NS, NS], [8, 8]], channel_multiplier=-1))
            seq(pl.tensor_tensor(low[:, :], low8[:, 0, :], low8[:, 1, :], ALU.add))
            pl.sem_inc(s_cst, 1)
            base = n[0]
            wkv(0)
            wkv(1)
            pl.memset(hq[:, :, :], 0.0).then_inc(s_zero, 1)

            def chunks_low(m):
                for q in SPLIT_AT.get(m, ()):
                    if q not in DVE_CHUNKS:
                        shared_weights_low(q)

            for s in range(B + 1):
                for c in range(NC):
                    m = NC * s + c
                    if m == 2 * NC - 1:
                        add_own(m)
                    if 1 <= m < NT - 1:
                        wkv(m + 1)
                    if s >= 1 and c == 0:
                        if s == B:
                            flat_low(m - 1)
                        if m < NT:
                            add_own(m)
                    if m == 2 * NC:
                        store_weights(0)
                    if c < 2 and 1 <= s < B:
                        for j in POSTS[s][c][:1]:
                            h_low(NJ * (s - 1) + j)
                    if m < NT and (s == 0 or c >= 1) and m != 2 * NC - 1:
                        add_own(m)
                    if s == 1:
                        chunks_low(m)
                    if 1 <= s < B:
                        for j in POSTS[s][c] if c >= 2 else POSTS[s][c][1:]:
                            h_low(NJ * (s - 1) + j)
                    if c >= 1 and m < NT:
                        flat_low(m - 1)
                    if s != 1:
                        chunks_low(m)
                    if 2 <= s < B and c == 2:
                        store_weights(s - 1)

            def copy_index(dst, src, at, count):
                pl.tensor_copy(dst, src[:, bass.ds(at, NS)]).then_inc(s_ix, 1)
                pl.wait_ge(s_ix, count)

            def gather(e, i, u, count):
                if not (isinstance(e, int) and e < RAW):
                    pl.wait_ge(s_tr, 2 * (e - RAW) + 2)
                    pl.wait_ge(s_wx, e - RAW + 1)
                if not (isinstance(e, int) and e < 2):
                    pl.wait_ge(s_xg[(u - 2) % RAW], (i + (u - 2) // RAW + 1) * 32)
                copy_index(gi[:, u % 2, :], tgat, e * NS, count)
                pl.sem_inc(s_go, 1)
                for h in range(NS):
                    pl.indirect_dma_start(xe[:, u, h, :], None, rows[:, :],
                                          bass.IndirectOffsetOnAxis(ap=gi[:, u % 2, h:h + 1], axis=0)).then_inc(s_xg[u], 16)

            def add_result(e, i, u, count):
                if not (isinstance(e, int) and e < 1):
                    pl.wait_ge(s_sc[(u - 1) % 2], (2 * (i + (u - 1) // PER) + ((u - 1) % PER) // 2 + 1) * 32)
                copy_index(si[:, u % 2, :], tscat, e * NS, count)
                for h in range(NS):
                    pl.wait_ge(s_y, 2 * e + h + 1)
                    pl.sem_inc(s_go, 1)
                    pl.indirect_dma_start(out[:, :], bass.IndirectOffsetOnAxis(ap=si[:, u % 2, h:h + 1], axis=0),
                                          yb[:, 2 * (u % 2) + h, :], None, compute_op=ALU.add).then_inc(s_sc[u % 2], 16)

            for j in range(NJ):
                h_low(NJ * (B - 1) + j)
                if j == 4:
                    store_weights(B - 1)
                    pl.wait_ge(s_tab, 1)
                    pl.wait_ge(s_wst, 16 * B)
                    for x in (0, 1):
                        pl.wait_ge(s_rowd[x], 16 * NI * B // 2)
                if 4 <= j < 4 + RAW - 1:
                    gather(j - 4, 0, j - 4, base + j - 3)
            for i in range(NI):
                pl.wait_ge(s_out[i], 16 * B)
            pl.wait_ge(s_zst, 16)

            def step(e, i, u):
                if isinstance(e, int):
                    done = base + RAW - 1 + max(0, min(e, E - 3)) + max(0, e - 1)
                else:
                    done = e * 2 + (base + 2)
                if has(e, 3) and not (isinstance(e, int) and e < 0):
                    gather(e + 3, i + (u + 3) // PER, (u + 3) % PER, done + 1)
                    done = done + 1
                if has(e, -1):
                    add_result(e - 1, i + (u - 1) // PER, (u - 1) % PER, done + 1)

            turns(pl, step)
            for x in (0, 1):
                pl.wait_ge(s_sc[x], 32 * E // 2)


def kernel(**inputs):
    import numpy as np
    import concourse.bacc as bacc
    from concourse.bass_utils import run_bass_kernel_spmd

    a = {k: np.asarray(v) for k, v in inputs.items()}
    x, side = a["x"], a["fside_BxSxS_0"]
    up, down = a["L0_ffn_up_w"], a["L0_ffn_down_w"]
    arrays = {
        "xT": np.transpose(x, (2, 0, 1)),
        "kT": np.transpose(side, (2, 0, 1)),
        "xrow": x.reshape(NTOK, C),
        "cond": a["cond_512"],
        "wdec": a["L0_cond_w"].reshape(NC, P).T,
        "ubon": a["L0_cond_u"].reshape(NC, P).T,
        "gateT": a["L0_ffn_gate_w"].T.reshape(NC, P, E).transpose(1, 0, 2),
        "bias": a["L0_ffn_bias_corr"],
        "upT": up.transpose(0, 2, 1).reshape(E, NC, P, H).transpose(0, 2, 1, 3).reshape(E, P, NC * H),
        "downT": down.transpose(0, 2, 1).reshape(E, NH, P, C).transpose(0, 2, 1, 3).reshape(E, P, NH * C),
        "supT": a["L0_ffn_shared_up_w"].T.reshape(NC, P, HS).transpose(1, 0, 2),
        "sdownT": a["L0_ffn_shared_down_w"].T.reshape(NJ, P, C).transpose(1, 0, 2),
    }
    nc = bacc.Bacc("TRN2", target_bir_lowering=False, num_devices=1)
    given, args = {}, []
    for name, value in arrays.items():
        given[name] = np.ascontiguousarray(value)
        args.append(nc.dram_tensor(name, given[name].shape, FP, kind="ExternalInput").ap())
    out = nc.dram_tensor("out_rows", [NTOK + CAP, C], FP, kind="ExternalOutput").ap()
    adaln_moe_kernel(nc, *args, out)
    got = run_bass_kernel_spmd(nc, [given], core_ids=[0]).results[0]["out_rows"]
    return got[:NTOK].reshape(B, T, C)
```
